# Optimizing a Trainium2 kernel written in Bass

```python
import numpy as np
import jax
import jax.numpy as jnp

def _softmax(x, axis=-1):
    return jax.nn.softmax(x, axis=axis)

def _gelu(x):
    return jax.nn.gelu(x, approximate=True)

def _silu(x):
    return jax.nn.silu(x)

def _sigmoid(x):
    return jax.nn.sigmoid(x)

def _layernorm(x, axis=-1, eps=1e-05):
    m = jnp.mean(x, axis=axis, keepdims=True)
    v = jnp.var(x, axis=axis, keepdims=True)
    return (x - m) / jnp.sqrt(v + eps)

def _scatter_add(tgt, idx, src, axis=0):
    return tgt.at[idx].add(src)

def _segment_sum(src, seg, n):
    return jax.ops.segment_sum(src, seg, n)
kernel_name = 'mk_seq_postln_d2_jaxref_r4_0cb0ba'

def setup_inputs(seed: int=0):
    np.random.seed(seed)
    _w = jnp.asarray

    def _L0_attn_setup():
        import jax, jax.numpy as jnp
        import numpy as np
        import math

        def _alibi_slopes(n_heads):

            def pow2(n):
                start = 2 ** (-2 ** (-(math.log2(n) - 3)))
                return [start ** i for i in range(n)]
            if math.log2(n_heads).is_integer():
                slopes = pow2(n_heads)
            else:
                closest = 2 ** math.floor(math.log2(n_heads))
                slopes = pow2(closest) + _alibi_slopes(2 * closest).tolist()[0::2][:n_heads - closest]
            return np.asarray(slopes, dtype=np.float32)
        key = jax.random.key(seed)
        ks = jax.random.split(key, 4)
        B, L, D = (2, 512, 256)
        s = 1.0 / math.sqrt(D)
        return {'x': jax.random.normal(ks[0], (B, L, D), jnp.float32), 'Wqkv': jax.random.normal(ks[1], (D, 3 * D), jnp.float32) * s, 'bqkv': jnp.zeros((3 * D,), jnp.float32), 'Wout': jax.random.normal(ks[2], (D, D), jnp.float32) * s, 'bout': jnp.zeros((D,), jnp.float32)}
    _L0_attn_in = _L0_attn_setup()

    def _L0_ffn_setup():
        import jax, jax.numpy as jnp
        import numpy as np
        B, S, D = (8, 1024, 256)
        E, R, K = (6, 16, 2)
        key = jax.random.key(seed)
        ks = jax.random.split(key, 9)
        sc = 0.02
        return {'x': jax.random.normal(ks[0], (B, S, D), jnp.float32), 'base_W': jax.random.normal(ks[1], (D, D), jnp.float32) * sc, 'base_b': jax.random.normal(ks[2], (D,), jnp.float32) * sc, 'shared_A': jax.random.normal(ks[3], (R, D), jnp.float32) * sc, 'shared_B': jax.random.normal(ks[4], (D, R), jnp.float32) * sc, 'routed_A': jax.random.normal(ks[5], (E, R, D), jnp.float32) * sc, 'routed_B': jax.random.normal(ks[6], (E, D, R), jnp.float32) * sc, 'router_W': jax.random.normal(ks[7], (E, D), jnp.float32) * sc, 'router_b': jax.random.normal(ks[8], (E,), jnp.float32) * sc}
    _L0_ffn_in = _L0_ffn_setup()

    def _L1_attn_setup():
        import jax, jax.numpy as jnp
        import numpy as np
        NUM_HEADS = 16
        key = jax.random.key(seed)
        k1, k2, k3 = jax.random.split(key, 3)
        B, N, C = (4, 1024, 256)
        x = jax.random.normal(k1, (B, N, C), dtype=jnp.float32)
        w_qkv = jax.random.normal(k2, (C, 3 * C), dtype=jnp.float32) * (2.0 / (C + 3 * C)) ** 0.5
        w_proj = jax.random.normal(k3, (C, C), dtype=jnp.float32) * (1.0 / C) ** 0.5
        b_proj = jnp.zeros((C,), dtype=jnp.float32)
        return {'x': x, 'w_qkv': w_qkv, 'w_proj': w_proj, 'b_proj': b_proj}
    _L1_attn_in = _L1_attn_setup()

    def _L1_ffn_setup():
        import jax, jax.numpy as jnp
        import numpy as np
        D = 256
        H = 512
        E = 8
        TOP_K = 2
        N_SHARED = 1
        B, S = (2, 256)
        key = jax.random.key(seed)
        ks = jax.random.split(key, 12)
        sc = 0.02
        return {'hidden': jax.random.normal(ks[0], (B, S, D), jnp.float32), 'router_w': jax.random.normal(ks[1], (D, E), jnp.float32) * sc, 'router_b': jnp.zeros((E,), jnp.float32), 'sw1': jax.random.normal(ks[2], (D, H), jnp.float32) * sc, 'sb1': jnp.zeros((H,), jnp.float32), 'sw2': jax.random.normal(ks[3], (H, D), jnp.float32) * sc, 'sb2': jnp.zeros((D,), jnp.float32), 'rw1': jax.random.normal(ks[4], (E, D, H), jnp.float32) * sc, 'rb1': jnp.zeros((E, H), jnp.float32), 'rw2': jax.random.normal(ks[5], (E, H, D), jnp.float32) * sc, 'rb2': jnp.zeros((E, D), jnp.float32)}
    _L1_ffn_in = _L1_ffn_setup()
    _d = {'L0_attn_x': _L0_attn_in['x'], 'L0_attn_Wqkv': _L0_attn_in['Wqkv'], 'L0_attn_bqkv': _L0_attn_in['bqkv'], 'L0_attn_Wout': _L0_attn_in['Wout'], 'L0_attn_bout': _L0_attn_in['bout'], 'L0_ffn_base_W': _L0_ffn_in['base_W'], 'L0_ffn_base_b': _L0_ffn_in['base_b'], 'L0_ffn_shared_A': _L0_ffn_in['shared_A'], 'L0_ffn_shared_B': _L0_ffn_in['shared_B'], 'L0_ffn_routed_A': _L0_ffn_in['routed_A'], 'L0_ffn_routed_B': _L0_ffn_in['routed_B'], 'L0_ffn_router_W': _L0_ffn_in['router_W'], 'L0_ffn_router_b': _L0_ffn_in['router_b'], 'L1_attn_w_qkv': _L1_attn_in['w_qkv'], 'L1_attn_w_proj': _L1_attn_in['w_proj'], 'L1_attn_b_proj': _L1_attn_in['b_proj'], 'L1_ffn_router_w': _L1_ffn_in['router_w'], 'L1_ffn_router_b': _L1_ffn_in['router_b'], 'L1_ffn_sw1': _L1_ffn_in['sw1'], 'L1_ffn_sb1': _L1_ffn_in['sb1'], 'L1_ffn_sw2': _L1_ffn_in['sw2'], 'L1_ffn_sb2': _L1_ffn_in['sb2'], 'L1_ffn_rw1': _L1_ffn_in['rw1'], 'L1_ffn_rb1': _L1_ffn_in['rb1'], 'L1_ffn_rw2': _L1_ffn_in['rw2'], 'L1_ffn_rb2': _L1_ffn_in['rb2']}
    _x0 = _d['L0_attn_x']
    _d['L0_attn_x'] = jax.random.normal(jax.random.fold_in(jax.random.key(seed), 1), (8, 512, 256), dtype=_x0.dtype)
    del _x0
    return _d

def reference(L0_attn_x, L0_attn_Wqkv, L0_attn_bqkv, L0_attn_Wout, L0_attn_bout, L0_ffn_base_W, L0_ffn_base_b, L0_ffn_shared_A, L0_ffn_shared_B, L0_ffn_routed_A, L0_ffn_routed_B, L0_ffn_router_W, L0_ffn_router_b, L1_attn_w_qkv, L1_attn_w_proj, L1_attn_b_proj, L1_ffn_router_w, L1_ffn_router_b, L1_ffn_sw1, L1_ffn_sb1, L1_ffn_sw2, L1_ffn_sb2, L1_ffn_rw1, L1_ffn_rb1, L1_ffn_rw2, L1_ffn_rb2):

    def _L0_attn_ref(x, Wqkv, bqkv, Wout, bout):
        import jax, jax.numpy as jnp
        import numpy as np
        import math

        def _alibi_slopes(n_heads):

            def pow2(n):
                start = 2 ** (-2 ** (-(math.log2(n) - 3)))
                return [start ** i for i in range(n)]
            if math.log2(n_heads).is_integer():
                slopes = pow2(n_heads)
            else:
                closest = 2 ** math.floor(math.log2(n_heads))
                slopes = pow2(closest) + _alibi_slopes(2 * closest).tolist()[0::2][:n_heads - closest]
            return np.asarray(slopes, dtype=np.float32)
        n_heads = 16
        B, L, D = x.shape
        head_dim = D // n_heads
        qkv = (x @ Wqkv + bqkv).reshape(B, L, 3, n_heads, head_dim)
        q, k, v = (qkv[:, :, 0], qkv[:, :, 1], qkv[:, :, 2])
        scores = jnp.einsum('bqhd,bkhd->bhqk', q, k) / math.sqrt(head_dim)
        pos = jnp.arange(L)
        bias = -jnp.abs(pos[None, :] - pos[:, None]).astype(jnp.float32)
        slopes = jnp.asarray(_alibi_slopes(n_heads))
        scores = scores + slopes[None, :, None, None] * bias[None, None]
        probs = jax.nn.softmax(scores, axis=-1)
        out = jnp.einsum('bhqk,bkhd->bqhd', probs, v).reshape(B, L, D)
        return out @ Wout + bout

    def _L0_ffn_ref(x, base_W, base_b, shared_A, shared_B, routed_A, routed_B, router_W, router_b):
        import jax, jax.numpy as jnp
        import numpy as np
        B, S, D = (8, 1024, 256)
        E, R, K = (6, 16, 2)
        base_out = jax.lax.stop_gradient(jnp.einsum('bsi,oi->bso', x, base_W) + base_b)
        shared_out = jnp.einsum('bsr,or->bso', jnp.einsum('bsi,ri->bsr', x, shared_A), shared_B)
        logits = jnp.einsum('bsi,ei->bse', x, router_W) + router_b
        gate = jax.nn.softmax(logits, axis=-1)
        topk_w, topk_i = jax.lax.top_k(gate, K)
        sparse_w = jnp.sum(jax.nn.one_hot(topk_i, E, dtype=gate.dtype) * topk_w[..., None], axis=-2)
        sparse_w = sparse_w / (jnp.sum(sparse_w, axis=-1, keepdims=True) + 1e-06)
        h = jnp.einsum('bsi,eri->bser', x, routed_A)
        routed_outs = jnp.einsum('bser,eor->bseo', h, routed_B)
        routed_out = jnp.einsum('bseo,bse->bso', routed_outs, sparse_w)
        return base_out + shared_out + routed_out

    def _L1_attn_ref(x, w_qkv, w_proj, b_proj):
        import jax, jax.numpy as jnp
        import numpy as np
        NUM_HEADS = 16
        B, N, C = x.shape
        H = NUM_HEADS
        D = C // H
        qkv = (x @ w_qkv).reshape(B, N, 3, H, D).transpose(2, 0, 3, 1, 4)
        q, k, v = (qkv[0], qkv[1], qkv[2])
        q = jax.nn.elu(q) + 1.0
        k = jax.nn.elu(k) + 1.0
        kv = jnp.einsum('bhnd,bhne->bhde', k, v)
        numerator = jnp.einsum('bhnd,bhde->bhne', q, kv)
        sum_k = k.sum(axis=-2)
        denominator = jnp.einsum('bhnd,bhd->bhn', q, sum_k)[..., None]
        y = numerator / denominator
        y = y.transpose(0, 2, 1, 3).reshape(B, N, C)
        out = y @ w_proj + b_proj
        return out

    def _L1_ffn_ref(hidden, router_w, router_b, sw1, sb1, sw2, sb2, rw1, rb1, rw2, rb2):
        import jax, jax.numpy as jnp
        import numpy as np
        D = 256
        H = 512
        E = 8
        TOP_K = 2
        N_SHARED = 1
        B, S = (2, 256)
        b, s, d = hidden.shape
        T = b * s
        flat = hidden.reshape(T, d)
        router_logits = flat @ router_w + router_b
        router_probs = jax.nn.softmax(router_logits, axis=-1)
        topk_probs, topk_idx = jax.lax.top_k(router_probs, TOP_K)
        weights = jnp.zeros_like(router_probs).at[jnp.arange(T)[:, None], topk_idx].add(topk_probs)
        sh = jax.nn.gelu(flat @ sw1 + sb1, approximate=False)
        shared_out = (sh @ sw2 + sb2) / N_SHARED
        h1 = jax.nn.gelu(jnp.einsum('td,edh->teh', flat, rw1) + rb1[None], approximate=False)
        expert_out = jnp.einsum('teh,ehd->ted', h1, rw2) + rb2[None]
        mixed = jnp.einsum('ted,te->td', expert_out, weights)
        return (shared_out + mixed).reshape(b, s, d)
    x = L0_attn_x
    x = _layernorm(x + _L0_attn_ref(x, L0_attn_Wqkv, L0_attn_bqkv, L0_attn_Wout, L0_attn_bout), axis=-1)
    x = _layernorm(x + _L0_ffn_ref(x, L0_ffn_base_W, L0_ffn_base_b, L0_ffn_shared_A, L0_ffn_shared_B, L0_ffn_routed_A, L0_ffn_routed_B, L0_ffn_router_W, L0_ffn_router_b), axis=-1)
    x = _layernorm(x + _L1_attn_ref(x, L1_attn_w_qkv, L1_attn_w_proj, L1_attn_b_proj), axis=-1)
    x = _layernorm(x + _L1_ffn_ref(x, L1_ffn_router_w, L1_ffn_router_b, L1_ffn_sw1, L1_ffn_sb1, L1_ffn_sw2, L1_ffn_sb2, L1_ffn_rw1, L1_ffn_rb1, L1_ffn_rw2, L1_ffn_rb2), axis=-1)
    return x

_drawn_inputs = setup_inputs


def setup_inputs(seed=0):
    import zlib

    import numpy as np

    out = dict(_drawn_inputs(seed))
    spreads = {'L0_attn_bqkv': (0.0, 0.1),
     'L0_attn_bout': (0.0, 0.1),
     'L1_attn_b_proj': (0.0, 0.1),
     'L1_ffn_router_b': (0.0, 0.464),
     'L1_ffn_sb1': (0.0, 0.338),
     'L1_ffn_sb2': (0.0, 0.1),
     'L1_ffn_rb1': (0.0, 0.8),
     'L1_ffn_rb2': (0.0, 0.314)}
    factors = {'L0_ffn_routed_A': 3.301,
     'L0_ffn_routed_B': 3.286,
     'L0_ffn_router_W': 4.031,
     'L0_ffn_router_b': 8.0,
     'L1_ffn_rw1': 2.867,
     'L1_ffn_rw2': 2.673}
    for name, (base, spread) in spreads.items():
        noise = np.random.default_rng([zlib.crc32(name.encode()), seed]).standard_normal(out[name].shape)
        drawn = base * np.exp(spread * noise) if base else spread * noise
        out[name] = jnp.asarray(drawn.astype(out[name].dtype))
    for name, factor in factors.items():
        out[name] = (out[name] * factor).astype(out[name].dtype)
    return out
```

```python
import math
from contextlib import ExitStack

import numpy as np

import concourse.bass as bass
from concourse import mybir

F32 = mybir.dt.float32
F32R = mybir.dt.float32r
F16 = mybir.dt.float16
I32 = mybir.dt.int32
U32 = mybir.dt.uint32
ACT = mybir.ActivationFunctionType
ALU = mybir.AluOpType
AX = mybir.AxisListType

B, L, D = 8, 512, 256
H, HD = 16, 16
P = 128
KT = L // P
KC = D // P
QUAD = 4
NQ = H // QUAD
HALF = L // 2
VW = 32
PAD = 96
NAL = 2 * KT * 2
MROW = PAD + NAL
SROWS = MROW + 1
TW = L + (KT - 1) * P

JOBS = {
    (0, 1): [("v", 1)], (0, 2): [("mt", 0)], (0, 3): [("xt", 0)], (0, 4): [("xt", 1)],
    (0, 5): [("ot", 0)], (0, 6): [("qk", 0)], (0, 7): [("qk", 1)],
    (1, 2): [("mt", 0)], (1, 3): [("qk", 2)], (1, 4): [("qk", 3)], (1, 5): [("ot", 0)],
    (2, 2): [("mt", 0)], (2, 3): [("v", 0)], (2, 5): [("ot", 0)],
    (3, 2): [("mt", 0)], (3, 5): [("ot", 0)],
}


def attention_phase(nc, ctx, block_ctx, a, ident, y_dram, slots_dram, zero_done):
    def sb(name, shape, dt):
        return ctx.enter_context(nc.sbuf_tensor(name, shape, dt))

    def sem(name):
        return ctx.enter_context(nc.semaphore(name))

    xin = sb("xin", [P, KT, D], F32)
    xT = sb("xT", [P, KC, L], F32)
    wqk = sb("wqk", [P, KC, 4, P], F32)
    wv = sb("wv", [P, KC, D], F32)
    bqk = sb("bqk", [P, 4], F32)
    bv = sb("bv", [P, D], F32)
    q32 = sb("q32", [P, 2, L], F32)
    qkhi = sb("qkhi", [P, 4, L], F32R)
    qklo = sb("qklo", [P, 4, L], F32R)
    qs = sb("qs", [P, H, L], F32R)
    ks = sb("ks", [P, H, L], F32R)
    near = sb("near", [P, 2, H, P], F32R)
    ident_r = sb("ident_r", [P, P], F32R)
    table = sb("table", [P, H, TW], F16)
    probs = sb("probs", [P, 2 * KT, 2 * L], F32)
    v = sb("v", [P, KT, H, VW], F32)
    biased = sb("biased", [P, 2, L], F16)
    mx = sb("mx", [P, 2, QUAD * KT], F32)
    mneg = sb("mneg", [QUAD * KT, 2, P], F32R)
    oT = sb("oT", [P, L], F32)
    rden = sb("rden", [P, KT, QUAD], F32)
    ys = sb("ys", [P, KT, D], F32)
    zeros = sb("zeros", [P, 1, D], F32)

    ps_sc = ctx.enter_context(nc.psum_tensor("ps_sc", [P, 2, 2 * L], F32))
    ps_mx = ctx.enter_context(nc.psum_tensor("ps_mx", [P, 2, L], F32))
    ps_o = ctx.enter_context(nc.psum_tensor("ps_o", [P, L], F32))
    ps_job = ctx.enter_context(nc.psum_tensor("ps_job", [P, L], F32))

    weights_in = sem("weights_in")
    tables_in = sem("tables_in")
    rows_in = sem("rows_in")
    x_in = sem("x_in")
    cleared = sem("cleared")
    full = {k: sem(f"{k}_full") for k in ("xt", "qk", "v", "mt", "ot")}
    free = {k: sem(f"{k}_free") for k in ("xt", "qk", "v", "mt", "ot")}
    hi_done = sem("hi_done")
    lo_done = sem("lo_done")
    stack_in = [sem(f"stack_in{q}") for q in range(NQ)]
    mrow_in = [sem(f"mrow_in{q}") for q in range(NQ)]
    scores_done = sem("scores_done")
    exp_done = sem("exp_done")
    mx_ready = sem("mx_ready")
    mx_done = sem("mx_done")
    pv_done = sem("pv_done")
    o_copied = sem("o_copied")
    rden_done = sem("rden_done")
    y_out = sem("y_out")
    row_max_may_run = sem("row_max_may_run")
    stack_is_free = sem("stack_is_free")

    block = block_ctx.enter_context(nc.Block())

    def job_index(kind, arg, b, qd):
        t = NQ * b + qd
        if kind == "v":
            return 2 * (b + 1) if arg == 0 else 2 * b + 1
        if kind == "xt":
            return 2 * (b + 1) + arg
        if kind == "qk":
            return 4 * (b + 1) + arg
        if kind == "mt":
            return t + 1
        return t - 1

    def jobs(qd, u, first, last):
        found = []
        for kind, arg in JOBS.get((qd, u), []):
            if last and (kind in ("xt", "qk") or (kind == "v" and arg == 0) or (kind == "mt" and qd == 3)):
                continue
            if first and qd == 0 and kind == "ot":
                continue
            found.append((kind, arg))
        return found

    def before(qd, u, b, first, last):
        s, w, bb, f = qd, u, b, first
        while True:
            w -= 1
            if w < 0:
                s, w = s - 1, 2 * KT - 1
                if s < 0:
                    if first:
                        return ("mt", 0)
                    return ("ot", job_index("ot", 0, b - 1, 3))
            got = jobs(s, w, f, last)
            if got:
                kind, arg = got[-1]
                return (kind, job_index(kind, arg, bb, s))

    def stack_loads(sp, b, q, first):
        g, r = q // 2, 64 * (q % 2)
        if not first:
            sp.wait_ge(scores_done, 2 * KT * (NQ * (b - 1) + q + 1))
            sp.sem_inc(stack_is_free, 1)
        sp.wait_ge(lo_done, 4 * b + 2 * g + 2)
        hs = slice(QUAD * q, QUAD * q + QUAD)
        for row, src, w in ((0, qkhi, 0), (1, qkhi, 0), (2, qklo, 0), (0, qkhi, 1), (1, qklo, 1), (2, qkhi, 1)):
            dst = (qs, ks)[w][HD * row:HD * row + HD, hs, :]
            sp.dma_start(dst.bitcast(F32), src[r:r + 64, 2 * g + w, :].bitcast(F32)).then_inc(stack_in[q], 16)

    def mrow_load(sp, b, q, t):
        sp.wait_ge(free["mt"], t + 1)
        sp.dma_start(qs[MROW:MROW + 1, QUAD * q:QUAD * q + QUAD, :].bitcast(F32),
                     mneg[:, q % 2, :].bitcast(F32)).then_inc(mrow_in[q], 16)

    def x_load(sp, b):
        sp.dma_start(xin[:, :, :], a["x"][b].rearrange("(i p) d -> p i d", p=P)).then_inc(x_in, 16)

    @block.sync
    def _(sp):
        x_load(sp, 0)
        sp.dma_start(ident[:, :], a["ident"]).then_inc(weights_in, 16)
        sp.dma_start(wqk[:, :, :, :], a["wqk"]).then_inc(weights_in, 16)
        sp.dma_start(wv[:, :, :], a["wv"]).then_inc(weights_in, 16)
        sp.dma_start(bqk[:, :], a["bqk"]).then_inc(weights_in, 16)
        sp.dma_start(bv[:, :], a["bv"].to_broadcast((P, D))).then_inc(weights_in, 16)
        sp.dma_start(table[:, :, :], a["table"]).then_inc(tables_in, 16)
        sp.wait_ge(cleared, 3)
        for q in range(NQ):
            stack_loads(sp, 0, q, True)
        sp.wait_ge(full["xt"], 2)
        x_load(sp, 1)
        mrow_load(sp, 0, 0, 0)

        def row(b, last):
            mrow_load(sp, b, 1, NQ * b + 1)
            if not last:
                stack_loads(sp, b + 1, 0, False)
            mrow_load(sp, b, 2, NQ * b + 2)
            if not last:
                stack_loads(sp, b + 1, 1, False)
            mrow_load(sp, b, 3, NQ * b + 3)
            if not last:
                stack_loads(sp, b + 1, 2, False)
                mrow_load(sp, b + 1, 0, NQ * b + 4)
                stack_loads(sp, b + 1, 3, False)

        row(0, False)
        with sp.Fori(1, B - 1) as b:
            sp.wait_ge(full["xt"], 2 * b + 2)
            x_load(sp, b + 1)
            row(b, False)
        row(B - 1, True)

    @block.gpsimd
    def _(pool):
        pool.memset(ks[0:PAD, :, :].bitcast(F32), 0.0).then_inc(cleared, 1)
        pool.dma_start(ident_r[:, :], a["ident"]).then_inc(rows_in, 16)
        pool.dma_start(ks[PAD:SROWS, :, :], a["k_rows"]).then_inc(rows_in, 16)
        pool.dma_start(qs[PAD:SROWS, :, :], a["q_rows"]).then_inc(rows_in, 16)
        pool.dma_start(near[:, :, :, :], a["near"]).then_inc(rows_in, 16)
        pool.memset(zeros[:, :, :], 0.0).then_inc(cleared, 1)

        def low(b, w):
            n = 4 * b + w
            pool.wait_ge(hi_done, n + 1)
            pool.tensor_tensor(qklo[:, w, :], q32[:, w % 2, :], qkhi[:, w, :], ALU.subtract).then_inc(lo_done, 1)

        def y_store(b):
            pool.wait_ge(free["ot"], NQ * (b + 1))
            pool.dma_start(y_dram[b].rearrange("(i p) d -> p i d", p=P), ys[:, :, :]).then_inc(y_out, 16)

        for w in range(4):
            low(0, w)
        for w in range(4):
            low(1, w)
        pool.wait_ge(cleared, 3)
        n = slots_dram.shape[0] // P
        pool.dma_start(slots_dram.rearrange("(j p) d -> p j d", p=P), zeros[:, :, :].to_broadcast((P, n, D))).then_inc(zero_done, 16)
        with pool.Fori(1, B - 1) as b:
            y_store(b - 1)
            for w in range(4):
                low(b + 1, w)
        y_store(B - 2)
        y_store(B - 1)
        pool.wait_ge(y_out, 16 * B)

    @block.tensor
    def _(pe):
        def job(kind, arg, n):
            if kind == "xt":
                pe.wait_ge(x_in, 16 * (n // 2 + 1) if isinstance(n, int) else (n - arg) * 8 + 16)
                for i in range(KT):
                    m = pe.transpose(ps_job[:, P * i:P * i + P], xin[:, i, P * arg:P * arg + P], ident[:, :])
            elif kind == "qk":
                pe.wait_ge(free["xt"], 2 * (n // 4 + 1) if isinstance(n, int) else (n - arg) // 2 + 2)
                for k in range(KC):
                    m = pe.matmul(ps_job[:, :], wqk[:, k, arg, :], xT[:, k, :], start=k == 0, stop=k == KC - 1)
            elif kind == "v":
                for i in range(KT):
                    for k in range(KC):
                        m = pe.matmul(ps_job[:, P * i:P * i + P], xT[:, k, P * i:P * i + P],
                                      wv[:, k, P * arg:P * arg + P], start=k == 0, stop=k == KC - 1)
            elif kind == "mt":
                pe.wait_ge(mx_done, 16 * n + 16)
                m = pe.transpose(ps_job[0:QUAD * KT, 0:P], mx[:, arg, :], ident[:, :])
            else:
                pe.wait_ge(o_copied, n + 1)
                for i in range(KT):
                    m = pe.transpose(ps_job[:, P * i:P * i + P], oT[:, P * i:P * i + P], ident[:, :])
            m.then_inc(full[kind], 1)

        def pv(t, q, kt, first):
            n = KT * t + kt
            pe.wait_ge(exp_done, 2 * n + 2)
            if kt == 0:
                if not first:
                    pe.wait_ge(o_copied, t)
            for j in range(QUAD):
                p = probs[:, 2 * kt + j // 2, :].rearrange("p (f a c) -> p f a c", f=2, a=2)[:, :, j % 2, :]
                m = pe.matmul(ps_o[VW * j:VW * j + VW, :].rearrange("p (f c) -> p f c", f=2), v[:, kt, QUAD * q + j, :], p,
                              start=kt == 0, stop=kt == KT - 1)
            m.then_inc(pv_done, 1)

        def scores(b, q, u, first):
            n = 2 * KT * (NQ * b + q) + u
            kt, pr = u // 2, u % 2
            if u == 0:
                pe.wait_ge(mrow_in[q], 16 * b + 16)
            if not (first and q == 0 and u < 2):
                pe.wait_ge(exp_done, n - 1)
            for f in range(2):
                for s in range(2):
                    h = QUAD * q + 2 * pr + s
                    pe.matmul(ps_sc[:, u % 2, L * f + HALF * s:L * f + HALF * s + HALF],
                              ks[0:SROWS, h, P * kt:P * kt + P], qs[0:SROWS, h, HALF * f:HALF * f + HALF],
                              start=s == 0, stop=False, skip_group_check=True)
            f = kt // 2
            out = ps_sc[:, u % 2, L * f:L * f + L].rearrange("p (s c) -> p s c", s=2)[:, :, P * (kt % 2):P * (kt % 2) + P]
            h = QUAD * q + 2 * pr
            for part in range(2):
                m = pe.matmul(out, ident_r[:, :], near[:, part, h:h + 2, :], start=False, stop=part == 1,
                              skip_group_check=True)
            m.then_inc(scores_done, 1)

        def maxima(b, q, i, first):
            n = 16 * (NQ * b + q) + i
            if i == 0:
                pe.wait_ge(stack_in[q], 96 * b + 96)
            if not (first and q == 0 and i < 2):
                pe.wait_ge(mx_done, n - 1)
            h, qt = QUAD * q + i // KT, i % KT
            pe.matmul(ps_mx[:, i % 2, :], qs[0:PAD, h, P * qt:P * qt + P], ks[0:PAD, h, :],
                      start=True, stop=True).then_inc(mx_ready, 1)

        pe.wait_ge(weights_in, 80)
        prev = None
        for kind, arg, n in [("xt", 0, 0), ("xt", 1, 1)] + [("qk", w, w) for w in range(4)] + [("v", 0, 0)]:
            if prev:
                pe.wait_ge(free[prev[0]], prev[1] + 1)
            job(kind, arg, n)
            prev = (kind, n)
        pe.wait_ge(rows_in, 64)
        for q in range(2):
            for u in range(2 * KT):
                for i in (2 * u, 2 * u + 1):
                    maxima(0, q, i, True)
                if q == 1 and u == 2:
                    pe.wait_ge(free["v"], 1)
                    job("mt", 0, 0)

        def row(b, first, last):
            for q in range(NQ):
                t = NQ * b + q
                for u in range(2 * KT):
                    scores(b, q, u, first)
                    if q < 2 or not last:
                        for i in (2 * u, 2 * u + 1):
                            maxima(b if q < 2 else b + 1, (q + 2) % NQ, i, False)
                    if u == 1 and not (first and q == 0):
                        pv(t - 1, (q - 1) % NQ, KT - 1, False)
                    elif u % 2 and u > 1:
                        if u == 3 and q == 0:
                            pe.wait_ge(free["v"], 2 * b + 1)
                        if u == 3 and q == 2:
                            pe.wait_ge(free["v"], 2 * b + 2)
                        pv(t, q, u // 2 - 1, first and q == 0)
                    for kind, arg in jobs(q, u, first, last):
                        was, m = before(q, u, b, first, last)
                        pe.wait_ge(free[was], m + 1)
                        if kind == "mt":
                            arg = (q + 1) % 2
                        job(kind, arg, job_index(kind, arg if kind != "mt" else 0, b, q))

        row(0, True, False)
        with pe.Fori(1, B - 1) as b:
            row(b, False, False)
        row(B - 1, False, True)
        pv(NQ * B - 1, NQ - 1, KT - 1, False)
        pe.wait_ge(free["ot"], NQ * B - 1)
        job("ot", 0, NQ * B - 1)

    @block.scalar
    def _(act):
        def job(kind, arg, n, b):
            if kind == "xt":
                act.wait_ge(full["xt"], n + 1)
                act.copy(xT[:, arg, :], ps_job[:, :]).then_inc(free["xt"], 1)

        def high(b, w, first):
            n = 4 * b + w
            act.wait_ge(free["qk"], n + 1)
            if not first:
                for q in (2 * (w // 2), 2 * (w // 2) + 1):
                    act.wait_ge(stack_in[q], 96 * b)
            act.copy(qkhi[:, w, :], q32[:, w % 2, :]).then_inc(hi_done, 1)

        def o_copy(t, first):
            act.wait_ge(pv_done, KT * t + KT)
            if not first:
                act.wait_ge(full["ot"], t)
            act.copy(oT[:, :], ps_o[:, :]).then_inc(o_copied, 1)

        job("xt", 0, 0, 0)
        job("xt", 1, 1, 0)
        for w in range(4):
            high(0, w, True)

        def row(b, first, last):
            for q in range(NQ):
                for u in range(2 * KT):
                    n = 2 * KT * (NQ * b + q) + u
                    act.wait_ge(scores_done, n + 1)
                    if not (first and q == 0):
                        act.wait_ge(pv_done, KT * (NQ * b + q - 1) + u // 2 + 1)
                    act.activation(probs[:, u, :], ps_sc[:, u % 2, :], ACT.Exp).then_inc(exp_done, 1)
                    if u == 2 and not (first and q == 0):
                        o_copy(NQ * b + q - 1, first and q == 1)
                    for kind, arg in jobs(q, u, first, last):
                        if kind == "xt":
                            job(kind, arg, job_index(kind, arg, b, q), b)
                    if not last:
                        w = {(0, 7): 0, (1, 0): 1, (1, 4): 2, (1, 5): 3}.get((q, u))
                        if w is not None:
                            high(b + 1, w, False)

        row(0, True, False)
        with act.Fori(1, B - 1) as b:
            row(b, False, False)
        row(B - 1, False, True)
        o_copy(NQ * B - 1, False)

    @block.vector
    def _(dve):
        def job(kind, arg, n, b, q):
            dve.wait_ge(full[kind], n + 1)
            if kind == "qk":
                if not (isinstance(n, int) and n < 2):
                    dve.wait_ge(lo_done, n - 1)
                dve.tensor_scalar(q32[:, arg % 2, :], ps_job[:, :], bqk[:, arg:arg + 1], HD ** -0.5 if arg % 2 == 0 else 1.0,
                                  ALU.add, ALU.mult).then_inc(free["qk"], 1)
            elif kind == "v":
                if not (isinstance(n, int) and n < 2):
                    dve.wait_ge(pv_done, 2 * KT * (n - 1))
                out = v[:, :, 8 * arg:8 * arg + 8, 0:HD]
                src = ps_job[:, :].rearrange("p (i h c) -> p i h c", i=KT, h=8)
                bias = bv[:, P * arg:P * arg + P].rearrange("p (o h c) -> p o h c", o=1, h=8).to_broadcast((P, KT, 8, HD))
                dve.tensor_tensor(out, src, bias, ALU.add).then_inc(free["v"], 1)
            else:
                src = ps_job[:, :].rearrange("p (i j c) -> p i j c", i=KT, j=QUAD)
                dve.reciprocal(rden[:, :, :], src[:, :, :, HD]).then_inc(rden_done, 1)
                dve.wait_ge(rden_done, n + 1)
                if q == 0 and b is not None:
                    dve.wait_ge(y_out, 16 * b)
                out = ys[:, :, 64 * q:64 * q + 64].rearrange("p i (j c) -> p i j c", j=QUAD)
                den = rden[:, :, :].rearrange("p i (j o) -> p i j o", o=1).to_broadcast((P, KT, QUAD, HD))
                dve.tensor_tensor(out, src[:, :, :, 0:HD], den, ALU.mult).then_inc(free["ot"], 1)

        def negate(n, half, loaded):
            dve.wait_ge(full["mt"], n + 1)
            if loaded is not None:
                dve.wait_ge(mrow_in[loaded[0]], loaded[1])
            dve.tensor_scalar(mneg[:, half, :], ps_job[0:QUAD * KT, 0:P], -1.0, None, ALU.mult).then_inc(free["mt"], 1)

        def row_max(b, q, i, first):
            n = 16 * (NQ * b + q) + i
            h, qt = QUAD * q + i // KT, i % KT
            dve.wait_ge(mx_ready, n + 1)
            if i == 0 and not (first and q < 2):
                dve.wait_ge(full["mt"], NQ * b + q - 1)
            if not (first and q == 0 and i < 2):
                dve.wait_ge(mx_done, n - 1)
            dve.sem_inc(row_max_may_run, 1)
            off = P * (KT - 1 - qt)
            dve.tensor_tensor_reduce(biased[:, i % 2, :], ps_mx[:, i % 2, :], table[:, h, off:off + L], 1.0, -3.0e38,
                                     ALU.add, ALU.max, mx[:, q % 2, i:i + 1]).then_inc(mx_done, 1)

        dve.memset(qs[0:PAD, :, :].bitcast(F32), 0.0).then_inc(cleared, 1)
        dve.memset(v[:, :, :, :], 1.0)
        dve.wait_ge(weights_in, 80)
        for w in range(4):
            job("qk", w, w, 0, 0)
        dve.wait_ge(tables_in, 16)
        job("v", 0, 0, 0, 0)
        for q in range(2):
            for u in range(2 * KT):
                for i in (2 * u, 2 * u + 1):
                    row_max(0, q, i, True)
                if q == 1 and u == 2:
                    negate(0, 0, None)

        def row(b, first, last):
            for q in range(NQ):
                t = NQ * b + q
                for u in range(2 * KT):
                    if q < 2 or not last:
                        for i in (2 * u, 2 * u + 1):
                            row_max(b if q < 2 else b + 1, (q + 2) % NQ, i, first and q < 2)
                    for kind, arg in jobs(q, u, first, last):
                        n = job_index(kind, arg, b, q)
                        if kind == "mt":
                            was, wb = (q - 1, b) if q else (NQ - 1, b - 1)
                            negate(n, (q + 1) % 2, None if first and q == 0 else (was, 16 * wb + 16))
                        elif kind == "ot":
                            job("ot", 0, n, None if (first or (q > 1 or q == 0)) else b, (q - 1) % NQ)
                        elif kind != "xt":
                            job(kind, arg, n, b, q)

        row(0, True, False)
        with dve.Fori(1, B - 1) as b:
            row(b, False, False)
        row(B - 1, False, True)
        job("ot", 0, NQ * B - 1, None, 3)


def round12(x):
    x = np.asarray(x, np.float64)
    m, e = np.frexp(x)
    return np.ldexp(np.rint(m * 4096.0), e - 12).astype(np.float32)


def alibi_constants():
    start = 2 ** (-2 ** (-(math.log2(H) - 3)))
    slopes = np.asarray([start ** i for i in range(H)], np.float32)
    tok = np.arange(L)
    k_rows = np.zeros((SROWS - PAD, H, L), np.float32)
    q_rows = np.zeros((SROWS - PAD, H, L), np.float32)
    for kt in range(KT):
        mid = P * kt + P // 2
        sign = np.where(tok // P > kt, 1.0, np.where(tok // P < kt, -1.0, 0.0))
        here = (tok // P == kt)
        for h in range(H):
            s = float(slopes[h])
            qv = -s * sign * (tok - mid)
            kv = s * (tok - mid) * here
            qh, kh = round12(qv), round12(kv)
            r = 4 * kt
            q_rows[r, h], k_rows[r, h] = qh, here
            q_rows[r + 1, h], k_rows[r + 1, h] = round12(qv - qh), here
            q_rows[r + 2, h], k_rows[r + 2, h] = sign, kh
            q_rows[r + 3, h], k_rows[r + 3, h] = sign, round12(kv - kh)
    k_rows[NAL] = 1.0
    d = np.abs(np.arange(P)[:, None] - np.arange(P)[None, :]).astype(np.float32)
    near = -(slopes[None, :, None] * d[:, None, :])
    hi = round12(near)
    near2 = np.stack([hi, round12(near.astype(np.float64) - hi)], 1)
    far = np.abs(np.arange(P)[:, None] + (KT - 1) * P - np.arange(TW)[None, :]).astype(np.float32)
    table = (-(slopes[None, :, None] * far[:, None, :])).astype(np.float16)
    return k_rows, q_rows, near2, table


def layout_attention(i):
    w = np.asarray(i["L0_attn_Wqkv"])
    bq = np.asarray(i["L0_attn_bqkv"])
    cols = np.array([[(QUAD * (2 * g + s) + j) * HD + d for s in range(2) for d in range(HD) for j in range(QUAD)]
                     for g in range(2)])
    idx = np.stack([cols[0], D + cols[0], cols[1], D + cols[1]])
    wqk = np.ascontiguousarray(w[:, idx].reshape(KC, P, 4, P).transpose(1, 0, 2, 3))
    wv = np.ascontiguousarray(w[:, 2 * D:].reshape(KC, P, D).transpose(1, 0, 2))
    return wqk, wv, np.ascontiguousarray(bq[idx].T), np.ascontiguousarray(bq[None, 2 * D:])

E0, R0 = 6, 16
NA = R0 + E0 * R0
E1, F1 = 8, 512
G = H // KC
NB = P + G
LN_EPS = 1e-5
PAD_LOGIT = -1.0e30

BEHIND = {"A": 0, "B": 1, "C": 2, "D": 3}
FILLS = {
    "x3T": ("D", (0, 1)), "x2T": ("C", (0, 1)), "x1T": ("B", (0, 1)), "yT": ("A", (0, 1)),
    "q": ("C", (6, 7)), "kv": ("C", (2, 3, 4, 5)), "out": ("A", (6, 7)), "lora": ("B", (0,)),
    "route": ("D", (1,)), "state": ("C", (0,)), "ffn": ("B", (6, 7)), "hT": ("B", (1,)),
    "num": ("C", (2, 3, 4, 5)), "y2T": ("C", (0, 1)), "proj": ("C", (6, 7)),
}
ORDER = list(FILLS)


def middle_phase(nc, ctx, block_ctx, a, ident, y_dram, x3_dram, gates_all, picks, loads_behind):
    def sb(name, shape, dt=F32):
        return ctx.enter_context(nc.sbuf_tensor(name, shape, dt))

    def sem(name):
        return ctx.enter_context(nc.semaphore(name))

    w_out = sb("w_out", [P, KC, D])
    w_lora = sb("w_lora", [P, KC, NA + E0])
    w_base = sb("w_base", [P, KC, D])
    w_up = sb("w_up", [NA, D])
    w_qkv1 = sb("w_qkv1", [P, KC, 3 * D])
    w_proj = sb("w_proj", [P, KC, D])
    w_route = sb("w_route", [P, KC, E1])
    b_out = sb("b_out", [P, 1, D])
    b_base = sb("b_base", [P, 1, D])
    b_proj = sb("b_proj", [P, 1, D])
    b_route0 = sb("b_route0", [P, 1, E0])
    b_route1 = sb("b_route1", [P, 1, E1])
    blocks = sb("blocks", [P, 1, NB])
    eps = sb("eps", [P, 1])
    lane = sb("lane", [P, 1, E1])

    y_in_sb = sb("y_in_sb", [P, KT, D])
    x_in_sb = sb("x_in_sb", [P, KT, D])
    yT = sb("yT", [P, KC, L])
    x3T = sb("x3T", [P, KC, L])
    x1T = sb("x1T", [P, KC, L])
    x2T = sb("x2T", [P, KC, L])
    y2T = sb("y2T", [P, KC, L])
    xb = {s: sb(f"xb_{s}", [P, KT, D]) for s in "ABC"}
    res = {s: sb(f"res_{s}", [P, KT, D]) for s in "ABC"}
    stats = {s: sb(f"stats_{s}", [P, KT, 6]) for s in "ABC"}
    mean_var = {s: sb(f"mean_var_{s}", [P, KT, 2]) for s in "ABC"}
    lnv = {s: sb(f"lnv_{s}", [P, KT]) for s in "ABC"}
    rstd = {s: sb(f"rstd_{s}", [P, KT]) for s in "ABC"}
    x = {s: sb(f"x_{s}", [P, KT, D]) for s in "ABC"}
    hid = sb("hid", [P, KT, NA])
    hT = sb("hT", [NA, L])
    gate = {s: {n: sb(f"{n}_{s}", [P, KT, E1]) for n in ("logit", "top", "shift", "ex", "pick0", "pick1", "mask", "kept", "w")}
            for s in "BD"}
    gate_idx = {s: sb(f"idx_{s}", [P, KT, 8], U32) for s in "BD"}
    gate_idf = {s: sb(f"idf_{s}", [P, KT, 2]) for s in "BD"}
    gate_sum = {s: sb(f"gsum_{s}", [P, KT, 4]) for s in "BD"}
    q_neg = sb("q_neg", [P, KC, L])
    q_exp = sb("q_exp", [P, KC, L])
    q_phi = sb("q_phi", [P, KC, L])
    k_neg = sb("k_neg", [P, KT, D])
    k_exp = sb("k_exp", [P, KT, D])
    k_phi = sb("k_phi", [P, KT, D])
    v1 = sb("v1", [P, KT, KC, P + 1])
    kv_bd = sb("kv_bd", [P, KC, NB])
    rden = sb("rden1", [P, KT, KC, G])
    y2 = sb("y2", [P, KT, D])
    ps = ctx.enter_context(nc.psum_tensor("ps_mid", [P, 8, L], F32))

    weights_in = sem("m_weights_in")
    ones_set = sem("m_ones_set")
    y_in = sem("m_y_in")
    x_in = sem("m_x_in")
    x3_out = sem("m_x3_out")
    waits_carried = sem("m_waits_carried")
    y_is_free = sem("m_y_is_free")
    full = {n: sem(f"m_full_{n}") for n in FILLS}
    free = {n: sem(f"m_free_{n}") for n in FILLS}
    xb_done = {s: sem(f"m_xb_done_{s}") for s in "ABC"}
    stats_done = {s: sem(f"m_stats_done_{s}") for s in "ABC"}
    mv_done = {s: sem(f"m_mv_done_{s}") for s in "ABC"}
    rstd_done = {s: sem(f"m_rstd_done_{s}") for s in "ABC"}
    x_done = {s: sem(f"m_x_done_{s}") for s in "ABC"}
    gate_step = {s: sem(f"m_gate_step_{s}") for s in "BD"}
    gate_exp = {s: sem(f"m_gate_exp_{s}") for s in "BD"}
    hid_done = sem("m_hid_done")
    neg_done = {n: sem(f"m_neg_done_{n}") for n in "qk"}
    exp_done = {n: sem(f"m_exp_done_{n}") for n in "qk"}
    v_done = sem("m_v_done")
    rden_done = sem("m_rden_done")
    ln_done = {s: sem(f"m_ln_done_{s}") for s in "ABC"}

    GSTEPS = 12
    RESIDUAL = {"A": "out", "B": "ffn", "C": "proj"}
    res_done = {s: free[name] for s, name in RESIDUAL.items()}

    def active(stage, i):
        return not isinstance(i, int) or 0 <= i - BEHIND[stage] < B

    def wait_bank(pe, name, part, i):
        bank = FILLS[name][1][part]
        k, it = ORDER.index(name) - 1, i
        for _ in range(2 * len(ORDER)):
            if k < 0:
                k, it = len(ORDER) - 1, it - 1
                if isinstance(it, int) and it < 0:
                    return
            was = ORDER[k]
            stage, banks = FILLS[was]
            if bank in banks and active(stage, it):
                pe.wait_ge(free[was], len(banks) * (it - BEHIND[stage]) + banks.index(bank) + 1)
                return
            k -= 1

    block = block_ctx.enter_context(nc.Block())
    WEIGHTS = [(w_out, "w_out"), (w_lora, "w_lora"), (w_base, "w_base"), (w_up, "w_up"), (w_qkv1, "w_qkv1"),
               (w_proj, "w_proj"), (w_route, "w_route"), (b_out, "b_out"), (b_base, "b_base"), (b_proj, "b_proj"),
               (b_route0, "b_route0"), (b_route1, "b_route1"), (blocks, "blocks"), (lane, "lane")]

    def iterations(eng, body):
        for i in range(4):
            body(i)
        with eng.Fori(4, B) as i:
            body(i)
        for i in range(B, B + 3):
            body(i)

    @block.sync
    def _(sp):
        def load(b):
            sp.dma_start(y_in_sb[:, :, :], y_dram[b].rearrange("(i p) d -> p i d", p=P)).then_inc(y_in, 16)
            sp.dma_start(x_in_sb[:, :, :], a["x"][b].rearrange("(i p) d -> p i d", p=P)).then_inc(x_in, 16)

        load(0)
        for t, name in WEIGHTS:
            src = a[name]
            if src.shape[0] == 1:
                src = src.to_broadcast(tuple(t.shape))
            sp.dma_start(t[tuple(slice(None) for _ in t.shape)], src).then_inc(weights_in, 16)

        def body(i):
            if active("D", i):
                b = i - 3
                sp.wait_ge(x_done["C"], b + 1)
                sp.dma_start(x3_dram[b].rearrange("(i p) d -> p i d", p=P), x["C"][:, :, :]).then_inc(x3_out, 16)
            if not isinstance(i, int) or i + 1 < B:
                sp.wait_ge(full["yT"], 2 * i + 2)
                sp.sem_inc(y_is_free, 1)
                sp.wait_ge(xb_done["A"], i + 1)
                load(i + 1)

        for i in range(4):
            body(i)
        with sp.Fori(4, B - 1) as i:
            body(i)
        for i in range(B - 1, B + 3):
            body(i)
        sp.wait_ge(x3_out, 16 * B)

    @block.gpsimd
    def _(pool):
        pool.memset(eps[:, :], LN_EPS).then_inc(ones_set, 1)
        pool.memset(v1[:, :, :, :], 1.0).then_inc(ones_set, 1)
        for s in "BD":
            pool.memset(gate[s]["logit"][:, :, :], PAD_LOGIT).then_inc(ones_set, 1)
        pool.wait_ge(weights_in, 16 * len(WEIGHTS))

        def biased(s, b, src, bias):
            if not (isinstance(b, int) and b == 0):
                pool.wait_ge(res_done[s], 2 * b)
            pool.tensor_tensor(xb[s][:, :, :], src[:, :, :], bias[:, :, :].to_broadcast((P, KT, D)), ALU.add).then_inc(xb_done[s], 1)

        for dst, src, s in loads_behind:
            pool.dma_start(dst, src).then_inc(s, 16)

        def body(i):
            if active("A", i):
                pool.wait_ge(x_in, 16 * i + 16)
                biased("A", i, x_in_sb, b_out)
            if active("B", i):
                pool.wait_ge(x_done["A"], i)
                biased("B", i - 1, x["A"], b_base)
            if active("C", i):
                pool.wait_ge(x_done["B"], i - 1)
                biased("C", i - 2, x["B"], b_proj)

        iterations(pool, body)

    @block.tensor
    def _(pe):
        def transposes(name, src, i):
            for k in range(KC):
                wait_bank(pe, name, k, i)
                for t in range(KT):
                    m = pe.transpose(ps[:, FILLS[name][1][k], P * t:P * t + P], src[:, t, P * k:P * k + P], ident[:, :])
                m.then_inc(full[name], 1)

        def two_per_bank(name, lhsT, w, i):
            for half in range(2):
                wait_bank(pe, name, half, i)
                bank = FILLS[name][1][half]
                for s in range(2):
                    t = 2 * half + s
                    for k in range(KC):
                        m = pe.matmul(ps[:, bank, D * s:D * s + D], lhsT[:, k, P * t:P * t + P], w[:, k, :],
                                      start=k == 0, stop=k == KC - 1)
                m.then_inc(full[name], 1)

        def body(i):
            if active("D", i):
                pe.wait_ge(x_done["C"], i - 2)
                transposes("x3T", x["C"], i)
            if active("C", i):
                pe.wait_ge(x_done["B"], i - 1)
                transposes("x2T", x["B"], i)
            if active("B", i):
                pe.wait_ge(x_done["A"], i)
                transposes("x1T", x["A"], i)
            if active("A", i):
                pe.wait_ge(y_in, 16 * i + 16)
                transposes("yT", y_in_sb, i)
            if active("C", i):
                b = i - 2
                pe.wait_ge(free["x2T"], 2 * b + 2)
                for c in range(KC):
                    wait_bank(pe, "q", c, i)
                    for k in range(KC):
                        m = pe.matmul(ps[:, FILLS["q"][1][c], :], w_qkv1[:, k, P * c:P * c + P], x2T[:, k, :],
                                      start=k == 0, stop=k == KC - 1)
                    m.then_inc(full["q"], 1)
                for t in range(KT):
                    wait_bank(pe, "kv", t, i)
                    for k in range(KC):
                        m = pe.matmul(ps[:, FILLS["kv"][1][t], :], x2T[:, k, P * t:P * t + P], w_qkv1[:, k, D:3 * D],
                                      start=k == 0, stop=k == KC - 1)
                    m.then_inc(full["kv"], 1)
            if active("A", i):
                pe.wait_ge(free["yT"], 2 * i + 2)
                two_per_bank("out", yT, w_out, i)
            if active("B", i):
                b = i - 1
                pe.wait_ge(free["x1T"], 2 * b + 2)
                wait_bank(pe, "lora", 0, i)
                for t in range(KT):
                    for k in range(KC):
                        m = pe.matmul(ps[:, FILLS["lora"][1][0], P * t:P * t + NA + E0], x1T[:, k, P * t:P * t + P],
                                      w_lora[:, k, :], start=k == 0, stop=k == KC - 1)
                m.then_inc(full["lora"], 1)
            if active("D", i):
                b = i - 3
                pe.wait_ge(free["x3T"], 2 * b + 2)
                wait_bank(pe, "route", 0, i)
                for t in range(KT):
                    for k in range(KC):
                        m = pe.matmul(ps[:, FILLS["route"][1][0], E1 * t:E1 * t + E1], x3T[:, k, P * t:P * t + P],
                                      w_route[:, k, :], start=k == 0, stop=k == KC - 1)
                m.then_inc(full["route"], 1)
            if active("C", i):
                b = i - 2
                wait_bank(pe, "state", 0, i)
                pe.wait_ge(free["kv"], 4 * b + 4)
                for c in range(KC):
                    for t in range(KT):
                        m = pe.matmul(ps[:, FILLS["state"][1][0], 256 * c:256 * c + P + 1], k_phi[:, t, P * c:P * c + P],
                                      v1[:, t, c, :], start=t == 0, stop=t == KT - 1)
                m.then_inc(full["state"], 1)
            if active("B", i):
                b = i - 1
                for half in range(2):
                    wait_bank(pe, "ffn", half, i)
                    bank = FILLS["ffn"][1][half]
                    for s in range(2):
                        t = 2 * half + s
                        for k in range(KC):
                            pe.matmul(ps[:, bank, D * s:D * s + D], x1T[:, k, P * t:P * t + P], w_base[:, k, :],
                                      start=k == 0 and s == 0, stop=False, skip_group_check=True)
                wait_bank(pe, "hT", 0, i)
                pe.wait_ge(hid_done, b + 1)
                for t in range(KT):
                    m = pe.transpose(ps[0:NA, FILLS["hT"][1][0], P * t:P * t + P], hid[:, t, :], ident[:, :])
                m.then_inc(full["hT"], 1)
            if active("C", i):
                b = i - 2
                pe.wait_ge(free["state"], b + 1)
                for t in range(KT):
                    wait_bank(pe, "num", t, i)
                    for c in range(KC):
                        m = pe.matmul(ps[:, FILLS["num"][1][t], NB * c:NB * c + NB], q_phi[:, c, P * t:P * t + P],
                                      kv_bd[:, c, :], start=True, stop=True)
                    m.then_inc(full["num"], 1)
            if active("B", i):
                b = i - 1
                pe.wait_ge(free["hT"], b + 1)
                for half in range(2):
                    bank = FILLS["ffn"][1][half]
                    for s in range(2):
                        t = 2 * half + s
                        m = pe.matmul(ps[:, bank, D * s:D * s + D], hT[:, P * t:P * t + P], w_up[:, :],
                                      start=False, stop=True, skip_group_check=True)
                    m.then_inc(full["ffn"], 1)
            if active("C", i):
                b = i - 2
                pe.wait_ge(free["num"], KT * (b + 1))
                transposes("y2T", y2, i)
                pe.wait_ge(free["y2T"], 2 * b + 2)
                two_per_bank("proj", y2T, w_proj, i)

        pe.wait_ge(weights_in, 16 * len(WEIGHTS))
        iterations(pe, body)

    @block.scalar
    def _(act):
        def evacuate(name, dst, i):
            b = i - BEHIND[FILLS[name][0]]
            for k in range(KC):
                act.wait_ge(full[name], KC * b + k + 1)
                act.copy(dst(b, k), ps[:, FILLS[name][1][k], :]).then_inc(free[name], 1)

        def positive(n, b, src, dst):
            act.wait_ge(neg_done[n], b + 1)
            act.activation(dst[:, :, :], src[:, :, :], ACT.Exp).then_inc(exp_done[n], 1)

        def inverse_std(s, b):
            act.wait_ge(mv_done[s], b + 1)
            act.activation(lnv[s][:, :], mean_var[s][:, :, 1], ACT.Ln, bias=eps[:, 0:1]).then_inc(ln_done[s], 1)
            act.wait_ge(ln_done[s], b + 1)
            act.activation(rstd[s][:, :], lnv[s][:, :], ACT.Exp, scale=-0.5).then_inc(rstd_done[s], 1)

        def gate_exponential(s, b):
            act.wait_ge(gate_step[s], GSTEPS * b + 3)
            act.activation(gate[s]["ex"][:, :, :], gate[s]["shift"][:, :, :], ACT.Exp).then_inc(gate_exp[s], 1)

        def body(i):
            if active("D", i):
                b = i - 3
                for k in range(KC):
                    act.wait_ge(full["x3T"], KC * b + k + 1)
                    if not (isinstance(b, int) and b == 0):
                        act.wait_ge(full["route"], b)
                    act.copy(x3T[:, k, :], ps[:, FILLS["x3T"][1][k], :]).then_inc(free["x3T"], 1)
            if active("C", i):
                evacuate("x2T", lambda b, k: x2T[:, k, :], i)
            if active("B", i):
                evacuate("x1T", lambda b, k: x1T[:, k, :], i)
            if active("A", i):
                evacuate("yT", lambda b, k: yT[:, k, :], i)
            if active("C", i):
                b = i - 2
                positive("q", b, q_neg, q_exp)
                for t in range(KT):
                    act.wait_ge(full["kv"], KT * b + t + 1)
                    act.copy(v1[:, t, :, 0:P], ps[:, FILLS["kv"][1][t], D:2 * D].rearrange("p (c f) -> p c f", c=KC)).then_inc(v_done, 1)
                positive("k", b, k_neg, k_exp)
            if active("A", i):
                inverse_std("A", i)
            if active("B", i):
                gate_exponential("B", i - 1)
            if active("D", i):
                gate_exponential("D", i - 3)
            if active("B", i):
                b = i - 1
                act.wait_ge(full["hT"], b + 1)
                act.copy(hT[:, :], ps[0:NA, FILLS["hT"][1][0], :]).then_inc(free["hT"], 1)
            if active("C", i):
                evacuate("y2T", lambda b, k: y2T[:, k, :], i)
            if active("B", i):
                inverse_std("B", i - 1)
            if active("C", i):
                inverse_std("C", i - 2)

        act.wait_ge(ones_set, 4)
        iterations(act, body)

    @block.vector
    def _(dve):
        def carry_waits():
            dve.sem_inc(waits_carried, 1)

        def phi(name, n, b, banks, neg, ex, out, w):
            src = ps[:, banks[0]:banks[-1] + 1, 0:w]
            dve.wait_ge(full[name], len(banks) * (b + 1))
            if name == "kv":
                dve.wait_ge(v_done, KT * (b + 1))
            dve.tensor_scalar(neg[:, :, :], src, 0.0, None, ALU.min).then_inc(neg_done[n], 1)
            dve.wait_ge(exp_done[n], b + 1)
            dve.scalar_tensor_tensor(out[:, :, :], src, 0.0, ex[:, :, :], ALU.max, ALU.add).then_inc(free[name], len(banks))

        def normalise(s, b, guard):
            name = RESIDUAL[s]
            dve.wait_ge(xb_done[s], b + 1)
            for half in range(2):
                dve.wait_ge(full[name], 2 * b + half + 1)
                dve.tensor_tensor(res[s][:, 2 * half:2 * half + 2, :],
                                  ps[:, FILLS[name][1][half], :].rearrange("p (t d) -> p t d", t=2),
                                  xb[s][:, 2 * half:2 * half + 2, :], ALU.add).then_inc(res_done[s], 1)
            for t in range(KT):
                dve.wait_ge(res_done[s], 2 * b + t // 2 + 1)
                dve.bn_stats(stats[s][:, t, :], res[s][:, t, :]).then_inc(stats_done[s], 1)
            for t in range(KT):
                dve.wait_ge(stats_done[s], KT * b + t + 1)
                carry_waits()
                m = dve.bn_aggr(mean_var[s][:, t, :], stats[s][:, t, :])
            m.then_inc(mv_done[s], 1)
            dve.wait_ge(mv_done[s], b + 1)
            dve.wait_ge(rstd_done[s], b + 1)
            guard()
            for t in range(KT):
                m = dve.tensor_scalar(x[s][:, t, :], res[s][:, t, :], mean_var[s][:, t, 0:1], rstd[s][:, t:t + 1],
                                      ALU.subtract, ALU.mult)
            m.then_inc(x_done[s], 1)

        def gates(s, b, logits, bias, n, name):
            g, idx, idf, sums = gate[s], gate_idx[s], gate_idf[s], gate_sum[s]
            base = GSTEPS * b
            step = [0]

            def link(m):
                step[0] += 1
                m.then_inc(gate_step[s], 1)
                dve.wait_ge(gate_step[s], base + step[0])

            def per_token(t, w=E1):
                return t.to_broadcast((P, KT, w))

            m = dve.tensor_tensor(g["logit"][:, :, 0:n], logits, bias[:, :, :].to_broadcast((P, KT, n)), ALU.add)
            m.then_inc(free[name], 1)
            dve.wait_ge(free[name], b + 1)
            carry_waits()
            for t in range(KT):
                m = dve.max(g["top"][:, t, :], g["logit"][:, t, :])
            link(m)
            carry_waits()
            for t in range(KT):
                m = dve.max_index(idx[:, t, :], g["top"][:, t, :], g["logit"][:, t, :])
            link(m)
            link(dve.tensor_tensor(g["shift"][:, :, :], g["logit"][:, :, :], per_token(g["top"][:, :, 0:1]), ALU.subtract))
            link(dve.tensor_copy(idf[:, :, :], idx[:, :, 0:2]))
            for k in range(2):
                pick = picks[k][:, bass.ds(KT * b, KT), :] if s == "D" else g[f"pick{k}"][:, :, :]
                link(dve.tensor_tensor(pick, lane[:, :, :].to_broadcast((P, KT, E1)),
                                       per_token(idf[:, :, k:k + 1]), ALU.is_equal))
            first, second = ((picks[k][:, bass.ds(KT * b, KT), :] for k in range(2)) if s == "D"
                             else (g[f"pick{k}"][:, :, :] for k in range(2)))
            link(dve.tensor_tensor(g["mask"][:, :, :], first, second, ALU.add))
            dve.wait_ge(gate_exp[s], b + 1)
            link(dve.tensor_tensor(g["kept"][:, :, :], g["ex"][:, :, :], g["mask"][:, :, :], ALU.mult))
            dve.tensor_reduce(sums[:, :, 1], g["kept"][:, :, :], AX.X, ALU.add)
            link(dve.tensor_reduce(sums[:, :, 0], g["ex"][:, :, :], AX.X, ALU.add))
            if s == "B":
                link(dve.scalar_tensor_tensor(sums[:, :, 2], sums[:, :, 0], 1e-6, sums[:, :, 1], ALU.mult, ALU.add))
            else:
                link(dve.tensor_copy(sums[:, :, 2], sums[:, :, 0]))
            link(dve.reciprocal(sums[:, :, 3], sums[:, :, 2]))
            out = g["w"][:, :, :] if s == "B" else gates_all[:, bass.ds(KT * b, KT), :]
            link(dve.tensor_tensor(out, g["kept"][:, :, :], per_token(sums[:, :, 3:4]), ALU.mult))
            assert step[0] == GSTEPS

        def body(i):
            if active("C", i):
                b = i - 2
                phi("q", "q", b, FILLS["q"][1], q_neg, q_exp, q_phi, L)
                phi("kv", "k", b, FILLS["kv"][1], k_neg, k_exp, k_phi, D)
            if active("A", i):
                def guard():
                    if active("B", i):
                        dve.wait_ge(full["x1T"], 2 * i)
                        dve.wait_ge(xb_done["B"], i)
                normalise("A", i, guard)
            if active("B", i):
                b = i - 1
                dve.wait_ge(full["lora"], b + 1)
                if not (isinstance(b, int) and b == 0):
                    dve.wait_ge(full["hT"], b)
                src = ps[:, FILLS["lora"][1][0], :].rearrange("p (t c) -> p t c", t=KT)
                dve.tensor_copy(hid[:, :, :], src[:, :, 0:NA])
                gates("B", b, src[:, :, NA:NA + E0], b_route0, E0, "lora")
                dve.tensor_tensor(hid[:, :, R0:NA].rearrange("p t (e r) -> p t e r", e=E0),
                                  hid[:, :, R0:NA].rearrange("p t (e r) -> p t e r", e=E0),
                                  gate["B"]["w"][:, :, 0:E0].rearrange("p t (e o) -> p t e o", o=1).to_broadcast((P, KT, E0, R0)),
                                  ALU.mult).then_inc(hid_done, 1)
            if active("D", i):
                b = i - 3
                dve.wait_ge(full["route"], b + 1)
                src = ps[:, FILLS["route"][1][0], 0:KT * E1].rearrange("p (t e) -> p t e", t=KT)
                gates("D", b, src, b_route1, E1, "route")
            if active("C", i):
                b = i - 2
                dve.wait_ge(full["state"], b + 1)
                src = ps[:, FILLS["state"][1][0], :].rearrange("p (c f) -> p c f", c=KC)
                dve.tensor_tensor(kv_bd[:, :, 0:P], src[:, :, 0:P], blocks[:, :, 0:P].to_broadcast((P, KC, P)), ALU.mult)
                dve.tensor_tensor(kv_bd[:, :, P:NB], src[:, :, P:P + 1].to_broadcast((P, KC, G)),
                                  blocks[:, :, P:NB].to_broadcast((P, KC, G)), ALU.mult).then_inc(free["state"], 1)
                dve.wait_ge(full["num"], KT * (b + 1))
                num = ps[:, 2:6, 0:KC * NB].rearrange("p t (c f) -> p t c f", c=KC)
                dve.reciprocal(rden[:, :, :, :], num[:, :, :, P:NB]).then_inc(rden_done, 1)
                dve.wait_ge(rden_done, b + 1)
                if not (isinstance(b, int) and b == 0):
                    dve.wait_ge(full["y2T"], 2 * b)
                for t in range(KT):
                    m = dve.tensor_tensor(y2[:, t, :].rearrange("p (c h d) -> p c h d", c=KC, h=G),
                                          num[:, t, :, 0:P].rearrange("p c (h d) -> p c h d", h=G),
                                          rden[:, t, :, :].rearrange("p c (h o) -> p c h o", o=1).to_broadcast((P, KC, G, HD)),
                                          ALU.mult)
                    m.then_inc(free["num"], 1)
            if active("B", i):
                def guard():
                    if active("C", i):
                        dve.wait_ge(full["x2T"], 2 * (i - 1))
                        dve.wait_ge(xb_done["C"], i - 1)
                normalise("B", i - 1, guard)
            if active("C", i):
                def guard():
                    if active("D", i):
                        dve.wait_ge(full["x3T"], 2 * (i - 2))
                        dve.wait_ge(x3_out, 16 * (i - 2))
                normalise("C", i - 2, guard)

        dve.wait_ge(weights_in, 16 * len(WEIGHTS))
        dve.wait_ge(ones_set, 4)
        iterations(dve, body)


def layout_middle(i):
    def chunks(w):
        w = np.asarray(w)
        return np.ascontiguousarray(w.reshape(KC, P, w.shape[1]).transpose(1, 0, 2))

    n = {k: np.asarray(v) for k, v in i.items()}
    lora = np.concatenate([n["L0_ffn_shared_A"], n["L0_ffn_routed_A"].reshape(E0 * R0, D), n["L0_ffn_router_W"]]).T
    up = np.concatenate([n["L0_ffn_shared_B"].T, n["L0_ffn_routed_B"].transpose(0, 2, 1).reshape(E0 * R0, D)])
    f = np.arange(P)
    blocks = np.concatenate([f[:, None] // HD == f[None] // HD, f[:, None] // HD == np.arange(G)[None]], 1)
    return {
        "w_out": chunks(n["L0_attn_Wout"]), "w_lora": chunks(lora), "w_base": chunks(n["L0_ffn_base_W"].T),
        "w_up": np.ascontiguousarray(up), "w_qkv1": chunks(n["L1_attn_w_qkv"]), "w_proj": chunks(n["L1_attn_w_proj"]),
        "w_route": chunks(n["L1_ffn_router_w"]), "b_out": n["L0_attn_bout"][None, None], "b_base": n["L0_ffn_base_b"][None, None],
        "b_proj": n["L1_attn_b_proj"][None, None], "b_route0": n["L0_ffn_router_b"][None, None],
        "b_route1": n["L1_ffn_router_b"][None, None], "blocks": blocks.astype(np.float32)[:, None],
        "lane": np.ascontiguousarray(np.broadcast_to(np.arange(E1, dtype=np.float32), (1, 1, E1))),
    }

FC = F1 // P
TT = B * KT
TOP = 2
ROUTED = TOP * TT + E1
HEAD = TT // 2
TILES = TT + ROUTED
PAIRS = TILES // 2
R0P, R1P = HEAD // 2, (HEAD + ROUTED) // 2
GROUP = 4


def expert_phase(nc, ctx, block_ctx, a, ident, w1, w2, gates_all, picks, x3_dram, slots_dram, y_dram, zero_done, w_in, out):
    def sb(name, shape, dt=F32):
        return ctx.enter_context(nc.sbuf_tensor(name, shape, dt))

    def sem(name):
        return ctx.enter_context(nc.semaphore(name))

    b1 = sb("b1", [P, E1 + 1, F1])
    b2 = sb("b2", [P, E1 + 1, D])
    below = sb("below", [P, P])
    ones = sb("ones", [P, P])
    tile_no = sb("tile_no", [1, ROUTED, 1])
    x3 = sb("x3_all", [P, TT, D])
    acc = sb("acc", [P, TT, D])
    mask = sb("mask", [P, TT, E1])
    total = sb("total", [P, TT, E1])
    scan = sb("scan", [P, 2, TT, E1])
    where = sb("where", [P, TT, E1])
    chosen = sb("chosen", [P, TOP, TT, E1])
    slot_f = sb("slot_f", [P, TOP, TT])
    slot = sb("slot", [P, TOP, TT], I32)
    count_i = sb("count_i", [P, 2, E1], I32)
    count_f = sb("count_f", [P, 2, E1])
    ends = sb("ends", [P, 2, 1, E1])
    past = sb("past", [1, ROUTED, E1])
    tile_f = sb("tile_f", [1, 2, ROUTED])
    tile_expert = sb("tile_expert", [1, ROUTED], I32)
    xrow = sb("xrow", [P, 2, D])
    xT = sb("xT3", [P, KC, P])
    pre = sb("pre", [P, F1])
    hid = sb("hid3", [P, F1])
    hT = sb("hT3", [P, FC, P])
    yrow = sb("yrow", [P, 2, D])
    got = sb("got", [P, GROUP, TOP, D])
    mix = sb("mix", [P, GROUP, D])
    stats = sb("stats3", [P, GROUP, 6])
    mv = sb("mv3", [P, GROUP, 2])
    lnv = sb("lnv3", [P, GROUP])
    rstd = sb("rstd3", [P, GROUP])
    eps = sb("eps3", [P, 1])
    result = sb("result", [P, GROUP, D])
    weights_k = sb("weights_k", [P, TOP, TT])

    ps_x = ctx.enter_context(nc.psum_tensor("ps_x", [P, L], F32))
    ps_up = ctx.enter_context(nc.psum_tensor("ps_up", [P, 2, F1], F32))
    ps_h = ctx.enter_context(nc.psum_tensor("ps_h", [P, 2, F1], F32))
    ps_y = ctx.enter_context(nc.psum_tensor("ps_y", [P, 2, L], F32))
    ps_r = ctx.enter_context(nc.psum_tensor("ps_r", [P, 2, TT, E1], F32))

    tables_in = sem("e_tables_in")
    x3_in = sem("e_x3_in")
    set_up = sem("e_set_up")
    route = sem("e_route_step")
    ranks_full = sem("e_ranks_full")
    places = sem("e_places_done")
    table_done = sem("e_table_done")
    scattered = sem("e_scattered")
    x_in = [sem(f"e_x_in{p}") for p in range(2)]
    x_full = sem("e_x_full")
    x_free = sem("e_x_free")
    up_full = sem("e_up_full")
    up_free = sem("e_up_free")
    gelu_done = sem("e_gelu_done")
    h_full = sem("e_h_full")
    h_free = sem("e_h_free")
    y_full = sem("e_y_full")
    y_free = sem("e_y_free")
    y_half = sem("e_y_half")
    y_out = [sem(f"e_y_out{p}") for p in range(2)]
    gathered = [sem(f"e_gathered{t}") for t in range(GROUP)]
    mixed0 = sem("e_mixed0")
    mixed = sem("e_mixed")
    stats_done = sem("e_stats_done")
    mv_done = sem("e_mv_done")
    ln_done = sem("e_ln_done")
    rstd_done = sem("e_rstd_done")
    result_done = sem("e_result_done")
    result_out = sem("e_result_out")
    waits_carried = sem("e_waits_carried")

    block = block_ctx.enter_context(nc.Block())

    def routed(n):
        return HEAD <= n < HEAD + ROUTED

    def kind(p, lag):
        n = 2 * p - lag
        return None if n < 0 or n >= TILES else routed(n)

    def pairs(eng, body):
        body(0, 0)
        body(1, 1)
        with eng.Fori(2, R0P) as p:
            body(p, 2)
        body(R0P, R0P)
        body(R0P + 1, R0P + 1)
        with eng.Fori(R0P + 2, R1P) as p:
            body(p, R0P + 2)
        body(R1P, R1P)
        body(R1P + 1, R1P + 1)
        with eng.Fori(R1P + 2, PAIRS - 1) as p:
            body(p, R1P + 2)
        body(PAIRS - 1, PAIRS - 1)
        body(PAIRS, PAIRS)

    @block.sync
    def _(sp):
        sp.dma_start(below[:, :], a["below"]).then_inc(tables_in, 16)
        sp.dma_start(tile_no[:, :, :], a["tile_no"]).then_inc(tables_in, 16)
        sp.dma_start(b1[:, E1:, :], a["sb1"].to_broadcast((P, 1, F1))).then_inc(tables_in, 16)
        sp.dma_start(b2[:, E1:, :], a["sb2"].to_broadcast((P, 1, D))).then_inc(tables_in, 16)

        def x_load(par, n_half, src):
            sp.dma_start(xrow[:, par, :], src).then_inc(x_in[par], 16)

        def row_tile(t):
            return x3_dram[bass.ds(t * P, P), :]

        for par in range(2):
            x_load(par, 0, row_tile(par))
        sp.dma_start(x3[:, :, :], x3_dram.rearrange("(i p) d -> p i d", p=P)).then_inc(x3_in, 16)
        sp.dma_start(b1[:, 0:E1, :], a["rb1"].to_broadcast((P, E1, F1))).then_inc(tables_in, 16)
        sp.dma_start(b2[:, 0:E1, :], a["rb2"].to_broadcast((P, E1, D))).then_inc(tables_in, 16)

        def loads(p, to_routed, base):
            for par in range(2):
                sp.wait_ge(x_full, 2 * p + par + 1)
                n = 2 * p + 2 + par
                src = slots_dram[bass.ds((n - HEAD) * P, P), :] if to_routed else x3_dram[bass.ds((n - base) * P, P), :]
                x_load(par, p + 1, src)

        def stores(p):
            for par in range(2):
                n = 2 * p + par
                sp.wait_ge(y_free, n + 1)
                sp.dma_start(y_dram[bass.ds((n - HEAD) * P, P), :], yrow[:, par, :]).then_inc(y_out[par], 16)

        def result_store(g):
            sp.wait_ge(result_done, g + 1)
            sp.dma_start(out[bass.ds(g, 1)].rearrange("g t p d -> p (g t) d"), result[:, :, :]).then_inc(result_out, 16)

        with sp.Fori(0, R0P - 1) as p:
            loads(p, False, 0)
        sp.wait_ge(scattered, 16 * TOP * TT)
        loads(R0P - 1, True, 0)
        loads(R0P, True, 0)
        with sp.Fori(R0P + 1, R1P - 1) as p:
            loads(p, True, 0)
            stores(p - 1)
        loads(R1P - 1, False, ROUTED)
        stores(R1P - 2)
        loads(R1P, False, ROUTED)
        stores(R1P - 1)
        with sp.Fori(R1P + 1, PAIRS - 1) as p:
            loads(p, False, ROUTED)
            result_store(p - (R1P + 1))
        for g in (PAIRS - R1P - 2, PAIRS - R1P - 1):
            result_store(g)
        sp.wait_ge(result_out, 16 * (TT // GROUP))

    @block.gpsimd
    def _(pool):
        pool.memset(ones[:, :], 1.0).then_inc(set_up, 1)
        pool.memset(eps[:, :], LN_EPS).then_inc(set_up, 1)
        pool.wait_ge(x3_in, 16)
        pool.wait_ge(places, 1)
        pool.wait_ge(zero_done, 16)
        for i in range(TT):
            for k in range(TOP):
                pool.indirect_dma_start(slots_dram, bass.IndirectOffsetOnAxis(ap=slot[:, k, i:i + 1], axis=0),
                                        x3[:, i, :], None).then_inc(scattered, 16)
        for par in range(2):
            pool.wait_ge(y_out[par], 16 * (ROUTED // 2))
        for i in range(TT):
            g, t = i // GROUP, i % GROUP
            if g:
                pool.wait_ge(mixed, i - GROUP + 1)
            for k in range(TOP):
                pool.indirect_dma_start(got[:, t, k, :], None, y_dram,
                                        bass.IndirectOffsetOnAxis(ap=slot[:, k, i:i + 1], axis=0)).then_inc(gathered[t], 16)

    @block.tensor
    def _(pe):
        def expert(eng, n, is_routed):
            if not is_routed:
                return E1
            return eng.value_load(tile_expert[0:1, bass.ds(n - HEAD, 1)], min_val=0, max_val=E1 - 1)

        def transpose_x(n, par, half):
            pe.wait_ge(x_in[par], 16 * (half + 1))
            if not (isinstance(n, int) and n == 0):
                pe.wait_ge(x_free, n)
            for k in range(KC):
                m = pe.transpose(ps_x[:, P * k:P * k + P], xrow[:, par, P * k:P * k + P], ident[:, :])
            m.then_inc(x_full, 1)

        def up(n, par, e):
            pe.wait_ge(x_free, n + 1)
            if not (isinstance(n, int) and n < 2):
                pe.wait_ge(up_free, n - 1)
            for k in range(KC):
                m = pe.matmul(ps_up[:, par, :], xT[:, k, :], w1[:, e, k, :], start=k == 0, stop=k == KC - 1)
            m.then_inc(up_full, 1)

        def transpose_h(n, par):
            pe.wait_ge(gelu_done, n + 1)
            if not (isinstance(n, int) and n < 2):
                pe.wait_ge(h_free, n - 1)
            for c in range(FC):
                m = pe.transpose(ps_h[:, par, P * c:P * c + P], hid[:, P * c:P * c + P], ident[:, :])
            m.then_inc(h_full, 1)

        def down(n, par, e):
            pe.wait_ge(h_free, n + 1)
            if not (isinstance(n, int) and n < 2):
                pe.wait_ge(y_free, n - 1)
            for c in range(FC):
                m = pe.matmul(ps_y[:, par, 0:D], hT[:, c, :], w2[:, e, c, :], start=c == 0, stop=c == FC - 1)
            m.then_inc(y_full, 1)

        def body(p, q):
            for par in range(2):
                n, nq = 2 * p + par, 2 * q + par
                if kind(q, 0) is not None:
                    up(n, par, expert(pe, n, routed(nq)))
                if nq + 1 < TILES:
                    transpose_x(n + 1, (par + 1) % 2, p + par)
                if kind(q, 2) is not None:
                    down(n - 2, par, expert(pe, n - 2, routed(nq - 2)))
                if 0 <= nq - 1 < TILES:
                    transpose_h(n - 1, (par + 1) % 2)

        pe.wait_ge(w_in, 64)
        pe.wait_ge(set_up, 2)
        pe.wait_ge(tables_in, 96)
        for k, lhsT in enumerate((below, ones)):
            pe.wait_ge(route, 1)
            m = pe.matmul(ps_r[:, k, :, :], lhsT[:, :], mask[:, :, :], start=True, stop=True)
        m.then_inc(ranks_full, 1)
        transpose_x(0, 0, 0)

        def first_routed(p, q):
            if q == R0P:
                pe.wait_ge(table_done, 1)
            body(p, q)

        pairs(pe, first_routed)

    @block.scalar
    def _(act):
        def inverse_std(g):
            act.wait_ge(mv_done, g + 1)
            act.activation(lnv[:, :], mv[:, :, 1], ACT.Ln, bias=eps[:, 0:1]).then_inc(ln_done, 1)
            act.wait_ge(ln_done, g + 1)
            act.activation(rstd[:, :], lnv[:, :], ACT.Exp, scale=-0.5).then_inc(rstd_done, 1)

        def x_copy(n):
            act.wait_ge(x_full, n + 1)
            if not (isinstance(n, int) and n == 0):
                act.wait_ge(up_full, n)
            act.copy(xT[:, :, :], ps_x[:, 0:D].rearrange("p (k t) -> p k t", k=KC)).then_inc(x_free, 1)

        def gelu(n):
            act.wait_ge(up_free, n + 1)
            if not (isinstance(n, int) and n == 0):
                act.wait_ge(h_full, n)
            act.activation(hid[:, :], pre[:, :], ACT.Gelu).then_inc(gelu_done, 1)

        def h_copy(n, par):
            act.wait_ge(h_full, n + 1)
            if not (isinstance(n, int) and n == 0):
                act.wait_ge(y_full, n)
            act.copy(hT[:, :, :], ps_h[:, par, :].rearrange("p (c t) -> p c t", c=FC)).then_inc(h_free, 1)

        def body(p, q):
            for par in range(2):
                n, nq = 2 * p + par, 2 * q + par
                if nq + 1 < TILES:
                    x_copy(n + 1)
                if 0 <= nq - 1 < TILES:
                    h_copy(n - 1, (par + 1) % 2)
                if nq < TILES:
                    gelu(n)
            if q > R1P:
                inverse_std(p - (R1P + 1))

        act.wait_ge(set_up, 2)
        x_copy(0)
        pairs(act, body)

    @block.vector
    def _(dve):
        step = [0]

        def link(m):
            step[0] += 1
            m.then_inc(route, 1)
            dve.wait_ge(route, step[0])

        def routing():
            link(dve.tensor_tensor(mask[:, :, :], picks[0][:, :, :], picks[1][:, :, :], ALU.add))
            dve.wait_ge(ranks_full, 1)
            link(dve.tensor_copy(total[:, :, :], ps_r[:, 1, :, :]))
            src, d, k = total[:, :, :], 1, 0
            while d < TT:
                dst = scan[:, k, :, :]
                dve.tensor_copy(dst[:, 0:d, :], src[:, 0:d, :])
                link(dve.tensor_tensor(dst[:, d:TT, :], src[:, d:TT, :], src[:, 0:TT - d, :], ALU.add))
                src, d, k = dst, 2 * d, 1 - k
            link(dve.tensor_scalar(count_i[:, 0, :], src[:, TT - 1, :], float(P - 1), None, ALU.add))
            link(dve.tensor_single_scalar(count_i[:, 1, :], count_i[:, 0, :], P.bit_length() - 1, ALU.logical_shift_right))
            link(dve.tensor_copy(count_f[:, 0, :], count_i[:, 1, :]))
            prev, d, k = count_f[:, 0, :], 1, 0
            while d < E1:
                dst = ends[:, k, 0, :]
                dve.tensor_copy(dst[:, 0:d], prev[:, 0:d])
                link(dve.tensor_tensor(dst[:, d:E1], prev[:, d:E1], prev[:, 0:E1 - d], ALU.add))
                prev, d, k = dst, 2 * d, 1 - k
            last = ends[:, 1 - k, :, :]
            link(dve.tensor_tensor(count_f[:, 1, :], prev, count_f[:, 0, :], ALU.subtract))
            link(dve.tensor_scalar(count_f[:, 1, :], count_f[:, 1, :], float(P), None, ALU.mult))
            link(dve.tensor_tensor(where[:, :, :], ps_r[:, 0, :, :], src, ALU.add))
            link(dve.tensor_tensor(where[:, :, :], where[:, :, :], total[:, :, :], ALU.subtract))
            link(dve.tensor_tensor(where[:, :, :], where[:, :, :],
                                   count_f[:, 1:2, :].to_broadcast((P, TT, E1)), ALU.add))
            for k in range(TOP):
                link(dve.tensor_tensor(chosen[:, k, :, :], where[:, :, :], picks[k][:, :, :], ALU.mult))
                link(dve.tensor_reduce(slot_f[:, k, :], chosen[:, k, :, :], AX.X, ALU.add))
            dve.tensor_copy(slot[:, :, :], slot_f[:, :, :]).then_inc(places, 1)
            link(dve.tensor_tensor(past[:, :, :], tile_no[:, :, :].to_broadcast((1, ROUTED, E1)),
                                   last[0:1, :, :].to_broadcast((1, ROUTED, E1)), ALU.is_ge))
            link(dve.tensor_reduce(tile_f[:, 0, :], past[:, :, :], AX.X, ALU.add))
            link(dve.tensor_scalar(tile_f[:, 1, :], tile_f[:, 0, :], float(E1 - 1), None, ALU.min))
            dve.tensor_copy(tile_expert[:, :], tile_f[:, 1, :]).then_inc(table_done, 1)
            dve.wait_ge(table_done, 1)

        def expert(n, is_routed):
            if not is_routed:
                return slice(E1, E1 + 1)
            return bass.ds(dve.value_load(tile_expert[0:1, bass.ds(n - HEAD, 1)], min_val=0, max_val=E1 - 1), 1)

        def add_b1(n, par, e):
            dve.wait_ge(up_full, n + 1)
            if not (isinstance(n, int) and n == 0):
                dve.wait_ge(gelu_done, n)
            dve.tensor_tensor(pre[:, :].rearrange("p (o f) -> p o f", o=1), ps_up[:, par:par + 1, :], b1[:, e, :],
                              ALU.add).then_inc(up_free, 1)

        def finish_routed(n, par, e, early):
            dve.wait_ge(y_full, n + 1)
            if not early:
                dve.wait_ge(y_out[par], 8 * (n - par - HEAD))
            dve.tensor_tensor(yrow[:, par:par + 1, :], ps_y[:, par:par + 1, 0:D], b2[:, e, :], ALU.add).then_inc(y_free, 1)

        def finish_shared(n, par, t, behind):
            dve.wait_ge(y_full, n + 1)
            if behind:
                dve.wait_ge(y_out[par], 16 * (ROUTED // 2))
            dve.tensor_tensor(yrow[:, par:par + 1, :], ps_y[:, par:par + 1, 0:D], b2[:, E1:, :], ALU.add).then_inc(y_half, 1)
            dve.wait_ge(y_half, t + 1)
            dve.tensor_tensor(acc[:, bass.ds(t, 1), :], x3[:, bass.ds(t, 1), :], yrow[:, par:par + 1, :],
                              ALU.add).then_inc(y_free, 1)

        def mix_group(g):
            if not (isinstance(g, int) and g == 0):
                dve.wait_ge(result_done, g)
            for t in range(GROUP):
                i = GROUP * g + t
                dve.wait_ge(gathered[t], 32 * (g + 1))
                dve.scalar_tensor_tensor(mix[:, t:t + 1, :], got[:, t:t + 1, 0, :], wk(0, i), acc[:, bass.ds(i, 1), :],
                                         ALU.mult, ALU.add).then_inc(mixed0, 1)
            for t in range(GROUP):
                i = GROUP * g + t
                dve.wait_ge(mixed0, i + 1)
                dve.scalar_tensor_tensor(mix[:, t:t + 1, :], got[:, t:t + 1, 1, :], wk(1, i), mix[:, t:t + 1, :],
                                         ALU.mult, ALU.add).then_inc(mixed, 1)
            for t in range(GROUP):
                dve.wait_ge(mixed, GROUP * g + t + 1)
                dve.bn_stats(stats[:, t, :], mix[:, t, :]).then_inc(stats_done, 1)
            for t in range(GROUP):
                dve.wait_ge(stats_done, GROUP * g + t + 1)
                dve.sem_inc(waits_carried, 1)
                m = dve.bn_aggr(mv[:, t, :], stats[:, t, :])
            m.then_inc(mv_done, 1)

        def normalise_group(g):
            dve.wait_ge(mv_done, g + 1)
            dve.wait_ge(rstd_done, g + 1)
            if not (isinstance(g, int) and g == 0):
                dve.wait_ge(result_out, 16 * g)
            for t in range(GROUP):
                m = dve.tensor_scalar(result[:, t, :], mix[:, t, :], mv[:, t, 0:1], rstd[:, t:t + 1], ALU.subtract, ALU.mult)
            m.then_inc(result_done, 1)

        def wk(k, i):
            return weights_k[:, k, bass.ds(i, 1)]


        def body(p, q):
            if R1P < q < PAIRS:
                mix_group(p - (R1P + 1))
            for par in range(2):
                n, nq = 2 * p + par, 2 * q + par
                if nq < TILES:
                    add_b1(n, par, expert(n, routed(nq)))
                if nq >= 2:
                    if routed(nq - 2):
                        finish_routed(n - 2, par, expert(n - 2, True), nq - 2 < HEAD + 2)
                    else:
                        t = n - 2 if nq - 2 < HEAD else n - 2 - ROUTED
                        finish_shared(n - 2, par, t, nq - 2 >= HEAD)
            if q == PAIRS:
                dve.wait_ge(y_free, TILES)
                mix_group(p - (R1P + 1))
            if q > R1P:
                normalise_group(p - (R1P + 1))

        dve.wait_ge(set_up, 2)
        dve.wait_ge(tables_in, 96)
        routing()
        for k in range(TOP):
            dve.tensor_tensor(chosen[:, k, :, :], gates_all[:, :, :], picks[k][:, :, :], ALU.mult).then_inc(places, 1)
            dve.wait_ge(places, 2 + 2 * k)
            dve.tensor_reduce(weights_k[:, k, :], chosen[:, k, :, :], AX.X, ALU.add).then_inc(places, 1)
            dve.wait_ge(places, 3 + 2 * k)
        dve.wait_ge(x3_in, 16)
        pairs(dve, body)


def layout_experts(i):
    n = {k: np.asarray(v) for k, v in i.items()}
    w1 = n["L1_ffn_rw1"].reshape(E1, KC, P, F1).transpose(2, 0, 1, 3)
    w2 = n["L1_ffn_rw2"].reshape(E1, FC, P, D).transpose(2, 0, 1, 3)
    return {
        "rw1": np.ascontiguousarray(w1), "rw2": np.ascontiguousarray(w2),
        "sw1": np.ascontiguousarray(n["L1_ffn_sw1"].reshape(1, KC, P, F1).transpose(2, 0, 1, 3)),
        "sw2": np.ascontiguousarray(n["L1_ffn_sw2"].reshape(1, FC, P, D).transpose(2, 0, 1, 3)),
        "rb1": n["L1_ffn_rb1"][None], "rb2": n["L1_ffn_rb2"][None], "sb1": n["L1_ffn_sb1"][None, None], "sb2": n["L1_ffn_sb2"][None, None],
        "below": np.triu(np.ones((P, P), np.float32), 1), "tile_no": np.arange(ROUTED, dtype=np.float32)[None, :, None],
    }


def build_program(nc, a, out):
    with ExitStack() as ctx:
        y_dram = nc.dram_tensor("y_scratch", (B, L, D), F32, kind="Internal").ap()
        x3_dram = nc.dram_tensor("x3_scratch", (B, L, D), F32, kind="Internal").ap()
        slots_dram = nc.dram_tensor("slots_scratch", (ROUTED * P, D), F32, kind="Internal").ap()
        routed_dram = nc.dram_tensor("routed_scratch", (ROUTED * P, D), F32, kind="Internal").ap()
        ident = ctx.enter_context(nc.sbuf_tensor("ident", [P, P], F32))
        gates_all = ctx.enter_context(nc.sbuf_tensor("gates_all", [P, TT, E1], F32))
        picks = [ctx.enter_context(nc.sbuf_tensor(f"pick{k}_all", [P, TT, E1], F32)) for k in range(TOP)]
        zero_done = ctx.enter_context(nc.semaphore("zero_done"))
        experts_in = ctx.enter_context(nc.semaphore("experts_in"))
        with ExitStack() as mem, ExitStack() as block:
            attention_phase(nc, mem, block, a, ident, y_dram, slots_dram, zero_done)
        w1 = ctx.enter_context(nc.sbuf_tensor("expert_w1", [P, E1 + 1, KC, F1], F32))
        w2 = ctx.enter_context(nc.sbuf_tensor("expert_w2", [P, E1 + 1, FC, D], F32))
        loads_behind = [(w1[:, E1:], a["sw1"], experts_in), (w2[:, E1:], a["sw2"], experts_in),
                        (w1[:, 0:E1], a["rw1"], experts_in), (w2[:, 0:E1], a["rw2"], experts_in)]
        with ExitStack() as mem, ExitStack() as block:
            middle_phase(nc, mem, block, a, ident, y_dram, x3_dram, gates_all, picks, loads_behind)
        with ExitStack() as mem, ExitStack() as block:
            expert_phase(nc, mem, block, a, ident, w1, w2, gates_all, picks, x3_dram.rearrange("b l d -> (b l) d"),
                         slots_dram, routed_dram, zero_done, experts_in,
                         out.rearrange("b (t p) d -> b t p d", p=P))


def kernel(**inputs):
    import numpy as _np
    import concourse.bacc as _bacc
    from concourse import mybir as _mybir
    from concourse.bass_utils import run_bass_kernel_spmd as _run

    given = {k: _np.asarray(v) for k, v in inputs.items()}
    wqk, wv, bqk, bv = layout_attention(given)
    k_rows, q_rows, near, table = alibi_constants()
    arrays = {"x": given["L0_attn_x"], "ident": _np.eye(P, dtype=_np.float32), "wqk": wqk, "wv": wv, "bqk": bqk, "bv": bv,
              "k_rows": k_rows, "q_rows": q_rows, "near": near, "table": table}
    arrays.update(layout_middle(given))
    arrays.update(layout_experts(given))
    arrays = {f"in_{k}_dram": _np.ascontiguousarray(v) for k, v in arrays.items()}

    nc = _bacc.Bacc("TRN2", target_bir_lowering=False, num_devices=1)
    a = {k[3:-5]: nc.dram_tensor(k, v.shape, _mybir.dt.from_np(v.dtype), kind="ExternalInput").ap() for k, v in arrays.items()}
    out = nc.dram_tensor("out_dram", (B, L, D), _mybir.dt.float32, kind="ExternalOutput").ap()
    build_program(nc, a, out)
    r = _run(nc, [arrays], core_ids=[0])
    return r.results[0]["out_dram"]
```

```python
import math
from contextlib import ExitStack

import numpy as np

import concourse.bass as bass
from concourse import mybir

F32 = mybir.dt.float32
F32R = mybir.dt.float32r
F16 = mybir.dt.float16
I32 = mybir.dt.int32
U32 = mybir.dt.uint32
ACT = mybir.ActivationFunctionType
ALU = mybir.AluOpType
AX = mybir.AxisListType

B, L, D = 8, 512, 256
H, HD = 16, 16
P = 128
KT = L // P
KC = D // P
QUAD = 4
NQ = H // QUAD
HALF = L // 2
VW = 32
PAD = 96
NAL = 2 * KT * 2
MROW = PAD + NAL
SROWS = MROW + 1
RING = 3
PER_QUAD = QUAD * KT
TW = L + (KT - 1) * P

JOBS = {
    (0, 1): [("v", 1)], (0, 2): [("mt", 0)], (0, 3): [("xt", 0)], (0, 4): [("xt", 1)],
    (0, 5): [("ot", 0)], (0, 6): [("qk", 0)], (0, 7): [("qk", 1)],
    (1, 2): [("mt", 0)], (1, 4): [("qk", 2)], (1, 5): [("ot", 0)], (1, 7): [("qk", 3)],
    (2, 2): [("mt", 0)], (2, 3): [("v", 0)], (2, 5): [("ot", 0)],
    (3, 2): [("mt", 0)], (3, 5): [("ot", 0)],
}


def attention_phase(nc, ctx, block_ctx, a, ident, y_dram, slots_dram, zero_done):
    def sb(name, shape, dt):
        return ctx.enter_context(nc.sbuf_tensor(name, shape, dt))

    def sem(name):
        return ctx.enter_context(nc.semaphore(name))

    xin = sb("xin", [P, KT, D], F32)
    xT = sb("xT", [P, KC, L], F32)
    xhi = sb("xhi", [P, KC, L], F32R)
    xlo = sb("xlo", [P, KC, L], F32R)
    whi = sb("wqk_hi", [P, KC, 4, P], F32R)
    wlo = sb("wqk_lo", [P, KC, 4, P], F32R)
    wv = sb("wv", [P, KC, D], F32)
    bqk = sb("bqk", [P, 4], F32)
    bv = sb("bv", [P, D], F32)
    q32 = sb("q32", [P, 2, L], F32)
    qkhi = sb("qkhi", [P, 4, L], F32R)
    qklo = sb("qklo", [P, 4, L], F32R)
    qs = sb("qs", [P, H, L], F32R)
    ks = sb("ks", [P, H, L], F32R)
    near = sb("near", [P, 2, H, P], F32R)
    ident_r = sb("ident_r", [P, P], F32R)
    table = sb("table", [P, H, TW], F16)
    probs = sb("probs", [P, 2 * KT, 2 * L], F32)
    v = sb("v", [P, KT, H, VW], F32)
    biased = sb("biased", [P, 2, L], F16)
    mx = sb("mx", [P, 2, QUAD * KT], F32)
    mneg = sb("mneg", [QUAD * KT, 2, P], F32R)
    oT = sb("oT", [P, L], F32)
    rden = sb("rden", [P, KT, QUAD], F32)
    ys = sb("ys", [P, KT, D], F32)
    zeros = sb("zeros", [P, 1, D], F32)

    ps_sc = ctx.enter_context(nc.psum_tensor("ps_sc", [P, RING, L], F32))
    ps_mx = ctx.enter_context(nc.psum_tensor("ps_mx", [P, RING, L], F32))
    ps_o = ctx.enter_context(nc.psum_tensor("ps_o", [P, L], F32))
    ps_job = ctx.enter_context(nc.psum_tensor("ps_job", [P, L], F32))

    weights_in = sem("weights_in")
    tables_in = sem("tables_in")
    rows_in = sem("rows_in")
    x_in = sem("x_in")
    cleared = sem("cleared")
    full = {k: sem(f"{k}_full") for k in ("xt", "qk", "v", "mt", "ot")}
    free = {k: sem(f"{k}_free") for k in ("xt", "qk", "v", "mt", "ot")}
    w_parts = sem("w_parts")
    xhi_done = sem("xhi_done")
    xlo_done = sem("xlo_done")
    hi_done = sem("hi_done")
    lo_done = sem("lo_done")
    stack_in = [sem(f"stack_in{q}") for q in range(NQ)]
    mrow_in = [sem(f"mrow_in{q}") for q in range(NQ)]
    scores_done = sem("scores_done")
    exp_done = sem("exp_done")
    mx_ready = sem("mx_ready")
    mx_done = sem("mx_done")
    pv_done = sem("pv_done")
    o_copied = sem("o_copied")
    rden_done = sem("rden_done")
    y_out = sem("y_out")
    row_max_may_run = sem("row_max_may_run")
    stack_is_free = sem("stack_is_free")

    w_stage = probs[:, 0, :].rearrange("p (k w f) -> p k w f", k=KC, w=4)
    block = block_ctx.enter_context(nc.Block())

    def job_index(kind, arg, b, qd):
        t = NQ * b + qd
        if kind == "v":
            return 2 * (b + 1) if arg == 0 else 2 * b + 1
        if kind == "xt":
            return 2 * (b + 1) + arg
        if kind == "qk":
            return 4 * (b + 1) + arg
        if kind == "mt":
            return t + 1
        return t - 1

    def ring_bank(q, i):
        return (PER_QUAD * q + i) % RING

    def wait_ring(pe, done, b, q, i, start):
        pos = PER_QUAD * q + i
        if start and pos < RING:
            return
        n = NQ * PER_QUAD * b + pos
        assert NQ * PER_QUAD % RING == 1
        back = RING if pos >= RING else 1 if pos == 0 else RING + 1
        pe.wait_ge(done, n - back + 1)

    def jobs(qd, u, first, last):
        found = []
        for kind, arg in JOBS.get((qd, u), []):
            if last and (kind in ("xt", "qk") or (kind == "v" and arg == 0) or (kind == "mt" and qd == 3)):
                continue
            if first and qd == 0 and kind == "ot":
                continue
            found.append((kind, arg))
        return found

    def before(qd, u, b, first, last):
        s, w, bb, f = qd, u, b, first
        while True:
            w -= 1
            if w < 0:
                s, w = s - 1, 2 * KT - 1
                if s < 0:
                    if first:
                        return ("mt", 0)
                    return ("ot", job_index("ot", 0, b - 1, 3))
            got = jobs(s, w, f, last)
            if got:
                kind, arg = got[-1]
                return (kind, job_index(kind, arg, bb, s))

    def stack_loads(sp, b, q, first):
        g, r = q // 2, 64 * (q % 2)
        if not first:
            sp.wait_ge(scores_done, PER_QUAD * (NQ * (b - 1) + q + 1))
            sp.sem_inc(stack_is_free, 1)
        sp.wait_ge(lo_done, 4 * b + 2 * g + 2)
        hs = slice(QUAD * q, QUAD * q + QUAD)
        for row, src, w in ((0, qkhi, 0), (1, qkhi, 0), (2, qklo, 0), (0, qkhi, 1), (1, qklo, 1), (2, qkhi, 1)):
            dst = (qs, ks)[w][HD * row:HD * row + HD, hs, :]
            sp.dma_start(dst.bitcast(F32), src[r:r + 64, 2 * g + w, :].bitcast(F32)).then_inc(stack_in[q], 16)

    def mrow_load(sp, q, t):
        sp.wait_ge(free["mt"], t + 1)
        sp.dma_start(qs[MROW:MROW + 1, QUAD * q:QUAD * q + QUAD, :].bitcast(F32),
                     mneg[:, q % 2, :].bitcast(F32)).then_inc(mrow_in[q], 16)

    def x_load(sp, b):
        sp.dma_start(xin[:, :, :], a["x"][b].rearrange("(i p) d -> p i d", p=P)).then_inc(x_in, 16)

    @block.sync
    def _(sp):
        x_load(sp, 0)
        sp.dma_start(ident[:, :], a["ident"]).then_inc(weights_in, 16)
        sp.dma_start(w_stage, a["wqk"]).then_inc(weights_in, 16)
        sp.dma_start(wv[:, :, :], a["wv"]).then_inc(weights_in, 16)
        sp.dma_start(bqk[:, :], a["bqk"]).then_inc(weights_in, 16)
        sp.dma_start(bv[:, :], a["bv"].to_broadcast((P, D))).then_inc(weights_in, 16)
        sp.dma_start(table[:, :, :], a["table"]).then_inc(tables_in, 16)
        sp.wait_ge(cleared, 3)
        for q in range(NQ):
            stack_loads(sp, 0, q, True)
        sp.wait_ge(full["xt"], 2)
        x_load(sp, 1)
        mrow_load(sp, 0, 0)

        def row(b, last):
            mrow_load(sp, 1, NQ * b + 1)
            if not last:
                stack_loads(sp, b + 1, 0, False)
            mrow_load(sp, 2, NQ * b + 2)
            if not last:
                stack_loads(sp, b + 1, 1, False)
            mrow_load(sp, 3, NQ * b + 3)
            if not last:
                stack_loads(sp, b + 1, 2, False)
                mrow_load(sp, 0, NQ * b + 4)
                stack_loads(sp, b + 1, 3, False)

        row(0, False)
        with sp.Fori(1, B - 1) as b:
            sp.wait_ge(full["xt"], 2 * b + 2)
            x_load(sp, b + 1)
            row(b, False)
        row(B - 1, True)

    @block.gpsimd
    def _(pool):
        pool.memset(ks[0:PAD, :, :].bitcast(F32), 0.0).then_inc(cleared, 1)
        pool.dma_start(ident_r[:, :], a["ident"]).then_inc(rows_in, 16)
        pool.dma_start(ks[PAD:SROWS, :, :], a["k_rows"]).then_inc(rows_in, 16)
        pool.dma_start(qs[PAD:SROWS, :, :], a["q_rows"]).then_inc(rows_in, 16)
        pool.dma_start(near[:, :, :, :], a["near"]).then_inc(rows_in, 16)
        pool.memset(zeros[:, :, :], 0.0).then_inc(cleared, 1)

        def x_low(b):
            for k in range(KC):
                pool.wait_ge(xhi_done, KC * b + k + 1)
                pool.wait_ge(free["xt"], KC * b + k + 1)
                pool.tensor_tensor(xlo[:, k, :], xT[:, k, :], xhi[:, k, :], ALU.subtract).then_inc(xlo_done, 1)

        def low(b, w):
            n = 4 * b + w
            pool.wait_ge(hi_done, n + 1)
            pool.tensor_tensor(qklo[:, w, :], q32[:, w % 2, :], qkhi[:, w, :], ALU.subtract).then_inc(lo_done, 1)

        def y_store(b):
            pool.wait_ge(free["ot"], NQ * (b + 1))
            pool.dma_start(y_dram[b].rearrange("(i p) d -> p i d", p=P), ys[:, :, :]).then_inc(y_out, 16)

        def clear_slots(b):
            n = slots_dram.shape[0] // P // B
            pool.dma_start(slots_dram.rearrange("(b j p) d -> b p j d", p=P, b=B)[b],
                           zeros[:, :, :].to_broadcast((P, n, D))).then_inc(zero_done, 16)

        for b in range(2):
            x_low(b)
            for w in range(4):
                low(b, w)
        pool.wait_ge(cleared, 3)
        clear_slots(0)
        with pool.Fori(1, B - 1) as b:
            x_low(b + 1)
            y_store(b - 1)
            for w in range(4):
                low(b + 1, w)
            clear_slots(b)
        y_store(B - 2)
        clear_slots(B - 1)
        y_store(B - 1)
        pool.wait_ge(y_out, 16 * B)

    @block.tensor
    def _(pe):
        def job(kind, arg, n):
            if kind == "xt":
                pe.wait_ge(x_in, 16 * (n // 2 + 1) if isinstance(n, int) else (n - arg) * 8 + 16)
                for i in range(KT):
                    m = pe.transpose(ps_job[:, P * i:P * i + P], xin[:, i, P * arg:P * arg + P], ident[:, :])
            elif kind == "qk":
                parts = 2 * (n // 4 + 1) if isinstance(n, int) else (n - arg) // 2 + 2
                pe.wait_ge(xhi_done, parts)
                for k in range(KC):
                    pe.matmul(ps_job[:, :], whi[:, k, arg, :], xhi[:, k, :], start=k == 0, stop=False)
                    pe.matmul(ps_job[:, :], wlo[:, k, arg, :], xhi[:, k, :], start=False, stop=False)
                pe.wait_ge(xlo_done, parts)
                for k in range(KC):
                    m = pe.matmul(ps_job[:, :], whi[:, k, arg, :], xlo[:, k, :], start=False, stop=k == KC - 1)
            elif kind == "v":
                for i in range(KT):
                    for k in range(KC):
                        m = pe.matmul(ps_job[:, P * i:P * i + P], xT[:, k, P * i:P * i + P],
                                      wv[:, k, P * arg:P * arg + P], start=k == 0, stop=k == KC - 1)
            elif kind == "mt":
                pe.wait_ge(mx_done, 16 * n + 16)
                m = pe.transpose(ps_job[0:QUAD * KT, 0:P], mx[:, arg, :], ident[:, :])
            else:
                pe.wait_ge(o_copied, n + 1)
                for i in range(KT):
                    m = pe.transpose(ps_job[:, P * i:P * i + P], oT[:, P * i:P * i + P], ident[:, :])
            m.then_inc(full[kind], 1)

        def pv(t, q, kt, first):
            n = KT * t + kt
            pe.wait_ge(exp_done, 4 * n + 4)
            if kt == 0:
                if not first:
                    pe.wait_ge(o_copied, t)
            for j in range(QUAD):
                p = probs[:, 2 * kt + j // 2, :].rearrange("p (f a c) -> p f a c", f=2, a=2)[:, :, j % 2, :]
                m = pe.matmul(ps_o[VW * j:VW * j + VW, :].rearrange("p (f c) -> p f c", f=2), v[:, kt, QUAD * q + j, :], p,
                              start=kt == 0, stop=kt == KT - 1)
            m.then_inc(pv_done, 1)

        def scores(b, q, u, first):
            kt, pr = u // 2, u % 2
            if u == 0:
                pe.wait_ge(mrow_in[q], 16 * b + 16)
            for f in range(2):
                bank = ps_sc[:, ring_bank(q, 2 * u + f), :].rearrange("p (s c) -> p s c", s=2)
                wait_ring(pe, exp_done, b, q, 2 * u + f, first)
                for s in range(2):
                    h = QUAD * q + 2 * pr + s
                    m = pe.matmul(bank[:, s, :], ks[0:SROWS, h, P * kt:P * kt + P], qs[0:SROWS, h, HALF * f:HALF * f + HALF],
                                  start=s == 0, stop=f != kt // 2, skip_group_check=True)
                if f == kt // 2:
                    h = QUAD * q + 2 * pr
                    for part in range(2):
                        m = pe.matmul(bank[:, :, P * (kt % 2):P * (kt % 2) + P], ident_r[:, :], near[:, part, h:h + 2, :],
                                      start=False, stop=part == 1, skip_group_check=True)
                m.then_inc(scores_done, 1)

        def maxima(b, q, i, first):
            if i == 0:
                pe.wait_ge(stack_in[q], 96 * b + 96)
            wait_ring(pe, mx_done, b, q, i, first)
            h, qt = QUAD * q + i // KT, i % KT
            pe.matmul(ps_mx[:, ring_bank(q, i), :], qs[0:PAD, h, P * qt:P * qt + P], ks[0:PAD, h, :],
                      start=True, stop=True).then_inc(mx_ready, 1)

        pe.wait_ge(weights_in, 80)
        prev = None
        for kind, arg, n in [("xt", 0, 0), ("xt", 1, 1)] + [("qk", w, w) for w in range(4)] + [("v", 0, 0)]:
            if prev:
                pe.wait_ge(free[prev[0]], prev[1] + 1)
            if (kind, n) == ("qk", 0):
                pe.wait_ge(w_parts, 2)
            job(kind, arg, n)
            prev = (kind, n)
        pe.wait_ge(rows_in, 64)
        for q in range(2):
            for u in range(2 * KT):
                for i in (2 * u, 2 * u + 1):
                    maxima(0, q, i, True)
                if q == 1 and u == 2:
                    pe.wait_ge(free["v"], 1)
                    job("mt", 0, 0)

        def row(b, first, last):
            for q in range(NQ):
                t = NQ * b + q
                for u in range(2 * KT):
                    scores(b, q, u, first)
                    ahead = q < 2 or not last
                    if ahead:
                        maxima(b if q < 2 else b + 1, (q + 2) % NQ, 2 * u, False)
                    if u == 1 and not (first and q == 0):
                        pv(t - 1, (q - 1) % NQ, KT - 1, False)
                    elif u % 2 and u > 1:
                        if u == 3 and q == 0:
                            pe.wait_ge(free["v"], 2 * b + 1)
                        if u == 3 and q == 2:
                            pe.wait_ge(free["v"], 2 * b + 2)
                        pv(t, q, u // 2 - 1, first and q == 0)
                    for kind, arg in jobs(q, u, first, last):
                        was, m = before(q, u, b, first, last)
                        pe.wait_ge(free[was], m + 1)
                        if kind == "mt":
                            arg = (q + 1) % 2
                        job(kind, arg, job_index(kind, arg if kind != "mt" else 0, b, q))
                    if ahead:
                        maxima(b if q < 2 else b + 1, (q + 2) % NQ, 2 * u + 1, False)

        row(0, True, False)
        with pe.Fori(1, B - 1) as b:
            row(b, False, False)
        row(B - 1, False, True)
        pv(NQ * B - 1, NQ - 1, KT - 1, False)
        pe.wait_ge(free["ot"], NQ * B - 1)
        job("ot", 0, NQ * B - 1)

    @block.scalar
    def _(act):
        def x_copy(arg, n):
            act.wait_ge(full["xt"], n + 1)
            act.copy(xhi[:, arg, :], ps_job[:, :]).then_inc(xhi_done, 1)
            act.copy(xT[:, arg, :], ps_job[:, :]).then_inc(free["xt"], 1)

        def high(b, w, first):
            n = 4 * b + w
            act.wait_ge(free["qk"], n + 1)
            if not first:
                for q in (2 * (w // 2), 2 * (w // 2) + 1):
                    act.wait_ge(stack_in[q], 96 * b)
            act.copy(qkhi[:, w, :], q32[:, w % 2, :]).then_inc(hi_done, 1)

        def o_copy(t, first):
            act.wait_ge(pv_done, KT * t + KT)
            if not first:
                act.wait_ge(full["ot"], t)
            act.copy(oT[:, :], ps_o[:, :]).then_inc(o_copied, 1)

        act.preload_act_table_set("natural_log_exp_and_others")
        x_copy(0, 0)
        x_copy(1, 1)
        for w in range(4):
            high(0, w, True)

        def row(b, first, last):
            for q in range(NQ):
                for u in range(2 * KT):
                    for f in range(2):
                        act.wait_ge(scores_done, PER_QUAD * (NQ * b + q) + 2 * u + f + 1)
                        if f == 0 and not (first and q == 0):
                            act.wait_ge(pv_done, KT * (NQ * b + q - 1) + u // 2 + 1)
                        act.activation(probs[:, u, L * f:L * f + L], ps_sc[:, ring_bank(q, 2 * u + f), :],
                                       ACT.Exp).then_inc(exp_done, 1)
                    if u == 2 and not (first and q == 0):
                        o_copy(NQ * b + q - 1, first and q == 1)
                    for kind, arg in jobs(q, u, first, last):
                        if kind == "xt":
                            x_copy(arg, job_index(kind, arg, b, q))
                    if not last:
                        w = {(0, 7): 0, (1, 0): 1, (1, 5): 2, (2, 0): 3}.get((q, u))
                        if w is not None:
                            high(b + 1, w, False)

        row(0, True, False)
        with act.Fori(1, B - 1) as b:
            row(b, False, False)
        row(B - 1, False, True)
        o_copy(NQ * B - 1, False)

    @block.vector
    def _(dve):
        def job(kind, arg, n, b, q):
            dve.wait_ge(full[kind], n + 1)
            if kind == "qk":
                if not (isinstance(n, int) and n < 2):
                    dve.wait_ge(lo_done, n - 1)
                dve.tensor_scalar(q32[:, arg % 2, :], ps_job[:, :], bqk[:, arg:arg + 1], HD ** -0.5 if arg % 2 == 0 else 1.0,
                                  ALU.add, ALU.mult).then_inc(free["qk"], 1)
            elif kind == "v":
                if not (isinstance(n, int) and n < 2):
                    dve.wait_ge(pv_done, 2 * KT * (n - 1))
                out = v[:, :, 8 * arg:8 * arg + 8, 0:HD]
                src = ps_job[:, :].rearrange("p (i h c) -> p i h c", i=KT, h=8)
                bias = bv[:, P * arg:P * arg + P].rearrange("p (o h c) -> p o h c", o=1, h=8).to_broadcast((P, KT, 8, HD))
                dve.tensor_tensor(out, src, bias, ALU.add).then_inc(free["v"], 1)
            else:
                src = ps_job[:, :].rearrange("p (i j c) -> p i j c", i=KT, j=QUAD)
                dve.reciprocal(rden[:, :, :], src[:, :, :, HD]).then_inc(rden_done, 1)
                dve.wait_ge(rden_done, n + 1)
                if q == 0 and b is not None:
                    dve.wait_ge(y_out, 16 * b)
                out = ys[:, :, 64 * q:64 * q + 64].rearrange("p i (j c) -> p i j c", j=QUAD)
                den = rden[:, :, :].rearrange("p i (j o) -> p i j o", o=1).to_broadcast((P, KT, QUAD, HD))
                dve.tensor_tensor(out, src[:, :, :, 0:HD], den, ALU.mult).then_inc(free["ot"], 1)

        def negate(n, half, loaded):
            dve.wait_ge(full["mt"], n + 1)
            if loaded is not None:
                dve.wait_ge(mrow_in[loaded[0]], loaded[1])
            dve.tensor_scalar(mneg[:, half, :], ps_job[0:QUAD * KT, 0:P], -1.0, None, ALU.mult).then_inc(free["mt"], 1)

        def row_max(b, q, i, first):
            n = 16 * (NQ * b + q) + i
            h, qt = QUAD * q + i // KT, i % KT
            dve.wait_ge(mx_ready, n + 1)
            if i == 0 and not (first and q < 2):
                dve.wait_ge(full["mt"], NQ * b + q - 1)
            if not (first and q == 0 and i < 2):
                dve.wait_ge(mx_done, n - 1)
            dve.sem_inc(row_max_may_run, 1)
            off = P * (KT - 1 - qt)
            dve.tensor_tensor_reduce(biased[:, i % 2, :], ps_mx[:, ring_bank(q, i), :], table[:, h, off:off + L], 1.0, -3.0e38,
                                     ALU.add, ALU.max, mx[:, q % 2, i:i + 1]).then_inc(mx_done, 1)

        dve.memset(qs[0:PAD, :, :].bitcast(F32), 0.0).then_inc(cleared, 1)
        dve.memset(v[:, :, :, :], 1.0)
        dve.wait_ge(weights_in, 80)
        dve.tensor_copy(whi[:, :, :, :], w_stage).then_inc(w_parts, 1)
        dve.wait_ge(w_parts, 1)
        dve.tensor_tensor(wlo[:, :, :, :], w_stage, whi[:, :, :, :], ALU.subtract).then_inc(w_parts, 1)
        for w in range(4):
            job("qk", w, w, 0, 0)
        dve.wait_ge(tables_in, 16)
        job("v", 0, 0, 0, 0)
        for q in range(2):
            for u in range(2 * KT):
                for i in (2 * u, 2 * u + 1):
                    row_max(0, q, i, True)
                if q == 1 and u == 2:
                    negate(0, 0, None)

        def row(b, first, last):
            for q in range(NQ):
                t = NQ * b + q
                for u in range(2 * KT):
                    if q < 2 or not last:
                        for i in (2 * u, 2 * u + 1):
                            row_max(b if q < 2 else b + 1, (q + 2) % NQ, i, first and q < 2)
                    for kind, arg in jobs(q, u, first, last):
                        n = job_index(kind, arg, b, q)
                        if kind == "mt":
                            was, wb = (q - 1, b) if q else (NQ - 1, b - 1)
                            negate(n, (q + 1) % 2, None if first and q == 0 else (was, 16 * wb + 16))
                        elif kind == "ot":
                            job("ot", 0, n, None if (first or (q > 1 or q == 0)) else b, (q - 1) % NQ)
                        elif kind != "xt":
                            job(kind, arg, n, b, q)

        row(0, True, False)
        with dve.Fori(1, B - 1) as b:
            row(b, False, False)
        row(B - 1, False, True)
        job("ot", 0, NQ * B - 1, None, 3)


def round12(x):
    x = np.asarray(x, np.float64)
    m, e = np.frexp(x)
    return np.ldexp(np.rint(m * 4096.0), e - 12).astype(np.float32)


def alibi_constants():
    start = 2 ** (-2 ** (-(math.log2(H) - 3)))
    slopes = np.asarray([start ** i for i in range(H)], np.float32)
    tok = np.arange(L)
    k_rows = np.zeros((SROWS - PAD, H, L), np.float32)
    q_rows = np.zeros((SROWS - PAD, H, L), np.float32)
    for kt in range(KT):
        mid = P * kt + P // 2
        sign = np.where(tok // P > kt, 1.0, np.where(tok // P < kt, -1.0, 0.0))
        here = (tok // P == kt)
        for h in range(H):
            s = float(slopes[h])
            qv = -s * sign * (tok - mid)
            kv = s * (tok - mid) * here
            qh, kh = round12(qv), round12(kv)
            r = 4 * kt
            q_rows[r, h], k_rows[r, h] = qh, here
            q_rows[r + 1, h], k_rows[r + 1, h] = round12(qv - qh), here
            q_rows[r + 2, h], k_rows[r + 2, h] = sign, kh
            q_rows[r + 3, h], k_rows[r + 3, h] = sign, round12(kv - kh)
    k_rows[NAL] = 1.0
    d = np.abs(np.arange(P)[:, None] - np.arange(P)[None, :]).astype(np.float32)
    near = -(slopes[None, :, None] * d[:, None, :])
    hi = round12(near)
    near2 = np.stack([hi, round12(near.astype(np.float64) - hi)], 1)
    far = np.abs(np.arange(P)[:, None] + (KT - 1) * P - np.arange(TW)[None, :]).astype(np.float32)
    table = (-(slopes[None, :, None] * far[:, None, :])).astype(np.float16)
    return k_rows, q_rows, near2, table


def layout_attention(i):
    w = np.asarray(i["L0_attn_Wqkv"])
    bq = np.asarray(i["L0_attn_bqkv"])
    cols = np.array([[(QUAD * (2 * g + s) + j) * HD + d for s in range(2) for d in range(HD) for j in range(QUAD)]
                     for g in range(2)])
    idx = np.stack([cols[0], D + cols[0], cols[1], D + cols[1]])
    wqk = np.ascontiguousarray(w[:, idx].reshape(KC, P, 4, P).transpose(1, 0, 2, 3))
    wv = np.ascontiguousarray(w[:, 2 * D:].reshape(KC, P, D).transpose(1, 0, 2))
    return wqk, wv, np.ascontiguousarray(bq[idx].T), np.ascontiguousarray(bq[None, 2 * D:])

E0, R0 = 6, 16
NA = R0 + E0 * R0
E1, F1 = 8, 512
G = H // KC
NB = P + G
LN_EPS = 1e-5
PAD_LOGIT = -1.0e30

BEHIND = {"A": 0, "B": 1, "C": 2, "D": 3}
FILLS = {
    "x2T": ("C", (0, 1)), "x1T": ("B", (4, 5)), "yT": ("A", (2, 3)), "q": ("C", (6, 7)),
    "kv": ("C", (2, 3, 4, 5)), "x3T": ("D", (0, 1)), "out": ("A", (6, 7)), "lora": ("B", (0,)),
    "route": ("D", (1,)), "state": ("C", (2,)), "ffn": ("B", (6, 7)), "num": ("C", (2, 3, 4, 5)),
    "hT": ("B", (0,)), "y2T": ("C", (0, 1)), "proj": ("C", (6, 7)),
}
ORDER = list(FILLS)


def middle_phase(nc, ctx, block_ctx, a, ident, y_dram, x3_dram, gates_all, picks, loads_behind):
    def sb(name, shape, dt=F32):
        return ctx.enter_context(nc.sbuf_tensor(name, shape, dt))

    def sem(name):
        return ctx.enter_context(nc.semaphore(name))

    w_out = sb("w_out", [P, KC, D])
    w_lora = sb("w_lora", [P, KC, NA + E0])
    w_base = sb("w_base", [P, KC, D])
    w_up = sb("w_up", [NA, D])
    w_hi = sb("w_qkv1_hi", [P, KC, 3 * D], F32R)
    w_lo = sb("w_qkv1_lo", [P, KC, 3 * D], F32R)
    w_proj = sb("w_proj", [P, KC, D])
    w_route = sb("w_route", [P, KC, E1])
    b_out = sb("b_out", [P, 1, D])
    b_base = sb("b_base", [P, 1, D])
    b_proj = sb("b_proj", [P, 1, D])
    b_route0 = sb("b_route0", [P, 1, E0])
    b_route1 = sb("b_route1", [P, 1, E1])
    blocks = sb("blocks", [P, 1, NB])
    eps = sb("eps", [P, 1])
    lane = sb("lane", [P, 1, E1])

    y_in_sb = sb("y_in_sb", [P, KT, D])
    x_in_sb = sb("x_in_sb", [P, KT, D])
    yT = sb("yT", [P, KC, L])
    x3T = sb("x3T", [P, KC, L])
    x1T = sb("x1T", [P, KC, L])
    x2hi = sb("x2hi", [P, KC, L], F32R)
    x2lo = sb("x2lo", [P, KC, L], F32R)
    y2T = sb("y2T", [P, KC, L])
    xb = {s: sb(f"xb_{s}", [P, KT, D]) for s in "ABC"}
    res = {s: sb(f"res_{s}", [P, KT, D]) for s in "ABC"}
    stats = {s: sb(f"stats_{s}", [P, KT, 6]) for s in "ABC"}
    mean_var = {s: sb(f"mean_var_{s}", [P, KT, 2]) for s in "ABC"}
    lnv = {s: sb(f"lnv_{s}", [P, KT]) for s in "ABC"}
    rstd = {s: sb(f"rstd_{s}", [P, KT]) for s in "ABC"}
    x = {s: sb(f"x_{s}", [P, KT, D]) for s in "ABC"}
    hid = sb("hid", [P, KT, NA])
    hT = sb("hT", [NA, L])
    gate = {s: {n: sb(f"{n}_{s}", [P, KT, E1]) for n in ("logit", "top", "shift", "ex", "pick0", "pick1", "mask", "kept", "w")}
            for s in "BD"}
    gate_idx = {s: sb(f"idx_{s}", [P, KT, 8], U32) for s in "BD"}
    gate_idf = {s: sb(f"idf_{s}", [P, KT, 2]) for s in "BD"}
    gate_sum = {s: sb(f"gsum_{s}", [P, KT, 4]) for s in "BD"}
    q_neg = sb("q_neg", [P, KC, L])
    q_exp = sb("q_exp", [P, KC, L])
    q_phi = sb("q_phi", [P, KC, L])
    k_neg = sb("k_neg", [P, KT, D])
    k_phi = sb("k_phi", [P, KT, D])
    v1 = sb("v1", [P, KT, KC, P + 1])
    kv_bd = sb("kv_bd", [P, KC, NB])
    rden = sb("rden1", [P, KT, KC, G])
    y2 = sb("y2", [P, KT, D])
    ps = ctx.enter_context(nc.psum_tensor("ps_mid", [P, 8, L], F32))

    first_in = sem("m_first_in")
    weights_in = sem("m_weights_in")
    ones_set = sem("m_ones_set")
    y_in = sem("m_y_in")
    x_in = sem("m_x_in")
    x3_out = sem("m_x3_out")
    waits_carried = sem("m_waits_carried")
    x2hi_done = sem("m_x2hi_done")
    w_parts = sem("m_w_parts")
    y_is_free = sem("m_y_is_free")
    full = {n: sem(f"m_full_{n}") for n in FILLS}
    free = {n: sem(f"m_free_{n}") for n in FILLS}
    xb_done = {s: sem(f"m_xb_done_{s}") for s in "ABC"}
    stats_done = {s: sem(f"m_stats_done_{s}") for s in "ABC"}
    mv_done = {s: sem(f"m_mv_done_{s}") for s in "ABC"}
    rstd_done = {s: sem(f"m_rstd_done_{s}") for s in "ABC"}
    x_done = {s: sem(f"m_x_done_{s}") for s in "ABC"}
    gate_step = {s: sem(f"m_gate_step_{s}") for s in "BD"}
    gate_exp = {s: sem(f"m_gate_exp_{s}") for s in "BD"}
    hid_done = sem("m_hid_done")
    neg_done = {n: sem(f"m_neg_done_{n}") for n in "qk"}
    exp_done = {n: sem(f"m_exp_done_{n}") for n in "qk"}
    v_done = sem("m_v_done")
    rden_done = sem("m_rden_done")
    ln_done = {s: sem(f"m_ln_done_{s}") for s in "ABC"}

    GSTEPS = {"B": 13, "D": 11}
    RESIDUAL = {"A": "out", "B": "ffn", "C": "proj"}
    res_done = {s: free[name] for s, name in RESIDUAL.items()}

    def active(stage, i):
        return not isinstance(i, int) or 0 <= i - BEHIND[stage] < B

    def wait_bank(pe, name, part, i):
        bank = FILLS[name][1][part]
        k, it = ORDER.index(name) - 1, i
        for _ in range(2 * len(ORDER)):
            if k < 0:
                k, it = len(ORDER) - 1, it - 1
                if isinstance(it, int) and it < 0:
                    return
            was = ORDER[k]
            stage, banks = FILLS[was]
            if bank in banks and active(stage, it):
                pe.wait_ge(free[was], len(banks) * (it - BEHIND[stage]) + banks.index(bank) + 1)
                return
            k -= 1

    w_stage = [t.rearrange("p a b -> p (a b)")[:, 0:3 * D] for t in (q_neg[:, :, :], q_exp[:, :, :])]
    block = block_ctx.enter_context(nc.Block())
    FIRST = 2
    WEIGHTS = [(w_out, "w_out"), (b_out, "b_out"), (w_lora, "w_lora"), (w_base, "w_base"), (w_up, "w_up"),
               (w_proj, "w_proj"), (w_route, "w_route"), (b_base, "b_base"), (b_proj, "b_proj"),
               (b_route0, "b_route0"), (b_route1, "b_route1"), (blocks, "blocks"), (lane, "lane")]

    def iterations(eng, body, waits_from):
        eng.wait_ge(first_in, 16 * FIRST)
        for i in range(4):
            if i == waits_from:
                eng.wait_ge(weights_in, 16 * (len(WEIGHTS) - FIRST + KC))
            body(i)
        with eng.Fori(4, B) as i:
            body(i)
        for i in range(B, B + 3):
            body(i)

    @block.sync
    def _(sp):
        def load(b):
            sp.dma_start(y_in_sb[:, :, :], y_dram[b].rearrange("(i p) d -> p i d", p=P)).then_inc(y_in, 16)
            sp.dma_start(x_in_sb[:, :, :], a["x"][b].rearrange("(i p) d -> p i d", p=P)).then_inc(x_in, 16)

        load(0)
        for k, (t, name) in enumerate(WEIGHTS):
            src = a[name]
            if src.shape[0] == 1:
                src = src.to_broadcast(tuple(t.shape))
            sp.dma_start(t[tuple(slice(None) for _ in t.shape)], src).then_inc(first_in if k < FIRST else weights_in, 16)

        for k in range(KC):
            sp.dma_start(w_stage[k], a["w_qkv1"][:, k, :]).then_inc(weights_in, 16)

        def body(i):
            if active("D", i):
                b = i - 3
                sp.wait_ge(x_done["C"], b + 1)
                sp.dma_start(x3_dram[b].rearrange("(i p) d -> p i d", p=P), x["C"][:, :, :]).then_inc(x3_out, 16)
            if not isinstance(i, int) or i + 1 < B:
                sp.wait_ge(full["yT"], 2 * i + 2)
                sp.sem_inc(y_is_free, 1)
                sp.wait_ge(xb_done["A"], i + 1)
                load(i + 1)

        for i in range(4):
            body(i)
        with sp.Fori(4, B - 1) as i:
            body(i)
        for i in range(B - 1, B + 3):
            body(i)
        sp.wait_ge(x3_out, 16 * B)

    @block.gpsimd
    def _(pool):
        pool.memset(eps[:, :], LN_EPS).then_inc(ones_set, 1)
        pool.memset(v1[:, :, :, :], 1.0).then_inc(ones_set, 1)
        for s in "BD":
            pool.memset(gate[s]["logit"][:, :, :], PAD_LOGIT).then_inc(ones_set, 1)

        def biased(s, b, src, bias):
            if not (isinstance(b, int) and b == 0):
                pool.wait_ge(res_done[s], 2 * b)
            pool.tensor_tensor(xb[s][:, :, :], src[:, :, :], bias[:, :, :].to_broadcast((P, KT, D)), ALU.add).then_inc(xb_done[s], 1)

        def body(i):
            if isinstance(i, int) and i == 1:
                for dst, src, s in loads_behind:
                    pool.dma_start(dst, src).then_inc(s, 16)
            if active("A", i):
                pool.wait_ge(x_in, 16 * i + 16)
                biased("A", i, x_in_sb, b_out)
            if active("B", i):
                pool.wait_ge(x_done["A"], i)
                biased("B", i - 1, x["A"], b_base)
            if active("C", i):
                pool.wait_ge(x_done["B"], i - 1)
                biased("C", i - 2, x["B"], b_proj)

        iterations(pool, body, 1)

    @block.tensor
    def _(pe):
        def transposes(name, src, i):
            for k in range(KC):
                wait_bank(pe, name, k, i)
                for t in range(KT):
                    m = pe.transpose(ps[:, FILLS[name][1][k], P * t:P * t + P], src[:, t, P * k:P * k + P], ident[:, :])
                m.then_inc(full[name], 1)

        def two_per_bank(name, lhsT, w, i):
            for half in range(2):
                wait_bank(pe, name, half, i)
                bank = FILLS[name][1][half]
                for s in range(2):
                    t = 2 * half + s
                    for k in range(KC):
                        m = pe.matmul(ps[:, bank, D * s:D * s + D], lhsT[:, k, P * t:P * t + P], w[:, k, :],
                                      start=k == 0, stop=k == KC - 1)
                m.then_inc(full[name], 1)

        def body(i):
            if active("C", i):
                pe.wait_ge(x_done["B"], i - 1)
                transposes("x2T", x["B"], i)
            if active("B", i):
                pe.wait_ge(x_done["A"], i)
                transposes("x1T", x["A"], i)
            if active("A", i):
                pe.wait_ge(y_in, 16 * i + 16)
                transposes("yT", y_in_sb, i)
            if active("C", i):
                b = i - 2
                if isinstance(i, int) and b == 0:
                    pe.wait_ge(w_parts, 2 * KC)
                pe.wait_ge(x2hi_done, KC * b + KC)
                for c in range(KC):
                    wait_bank(pe, "q", c, i)
                    cut = slice(P * c, P * c + P)
                    for k in range(KC):
                        pe.matmul(ps[:, FILLS["q"][1][c], :], w_hi[:, k, cut], x2hi[:, k, :], start=k == 0, stop=False)
                        pe.matmul(ps[:, FILLS["q"][1][c], :], w_lo[:, k, cut], x2hi[:, k, :], start=False, stop=False)
                pe.wait_ge(free["x2T"], KC * b + KC)
                for c in range(KC):
                    cut = slice(P * c, P * c + P)
                    for k in range(KC):
                        m = pe.matmul(ps[:, FILLS["q"][1][c], :], w_hi[:, k, cut], x2lo[:, k, :], start=False, stop=k == KC - 1)
                    m.then_inc(full["q"], 1)
                for t in range(KT):
                    wait_bank(pe, "kv", t, i)
                    cut = slice(P * t, P * t + P)
                    for k in range(KC):
                        out = ps[:, FILLS["kv"][1][t], :]
                        pe.matmul(out, x2hi[:, k, cut], w_hi[:, k, D:3 * D], start=k == 0, stop=False)
                        pe.matmul(out, x2hi[:, k, cut], w_lo[:, k, D:3 * D], start=False, stop=False)
                        m = pe.matmul(out, x2lo[:, k, cut], w_hi[:, k, D:3 * D], start=False, stop=k == KC - 1)
                    m.then_inc(full["kv"], 1)
            if active("D", i):
                pe.wait_ge(x_done["C"], i - 2)
                transposes("x3T", x["C"], i)
            if active("A", i):
                pe.wait_ge(free["yT"], 2 * i + 2)
                two_per_bank("out", yT, w_out, i)
            if active("B", i):
                b = i - 1
                pe.wait_ge(free["x1T"], 2 * b + 2)
                wait_bank(pe, "lora", 0, i)
                for t in range(KT):
                    for k in range(KC):
                        m = pe.matmul(ps[:, FILLS["lora"][1][0], P * t:P * t + NA + E0], x1T[:, k, P * t:P * t + P],
                                      w_lora[:, k, :], start=k == 0, stop=k == KC - 1)
                m.then_inc(full["lora"], 1)
            if active("D", i):
                b = i - 3
                pe.wait_ge(free["x3T"], 2 * b + 2)
                wait_bank(pe, "route", 0, i)
                for t in range(KT):
                    for k in range(KC):
                        m = pe.matmul(ps[:, FILLS["route"][1][0], E1 * t:E1 * t + E1], x3T[:, k, P * t:P * t + P],
                                      w_route[:, k, :], start=k == 0, stop=k == KC - 1)
                m.then_inc(full["route"], 1)
            if active("C", i):
                b = i - 2
                wait_bank(pe, "state", 0, i)
                pe.wait_ge(free["kv"], 4 * b + 4)
                for c in range(KC):
                    for t in range(KT):
                        m = pe.matmul(ps[:, FILLS["state"][1][0], 256 * c:256 * c + P + 1], k_phi[:, t, P * c:P * c + P],
                                      v1[:, t, c, :], start=t == 0, stop=t == KT - 1)
                m.then_inc(full["state"], 1)
            if active("B", i):
                b = i - 1
                for half in range(2):
                    wait_bank(pe, "ffn", half, i)
                    bank = FILLS["ffn"][1][half]
                    for s in range(2):
                        t = 2 * half + s
                        for k in range(KC):
                            pe.matmul(ps[:, bank, D * s:D * s + D], x1T[:, k, P * t:P * t + P], w_base[:, k, :],
                                      start=k == 0 and s == 0, stop=False, skip_group_check=True)
            if active("C", i):
                b = i - 2
                pe.wait_ge(free["state"], b + 1)
                for t in range(KT):
                    wait_bank(pe, "num", t, i)
                    for c in range(KC):
                        m = pe.matmul(ps[:, FILLS["num"][1][t], NB * c:NB * c + NB], q_phi[:, c, P * t:P * t + P],
                                      kv_bd[:, c, :], start=True, stop=True)
                    m.then_inc(full["num"], 1)
            if active("B", i):
                b = i - 1
                wait_bank(pe, "hT", 0, i)
                pe.wait_ge(hid_done, b + 1)
                for t in range(KT):
                    m = pe.transpose(ps[0:NA, FILLS["hT"][1][0], P * t:P * t + P], hid[:, t, :], ident[:, :])
                m.then_inc(full["hT"], 1)
            if active("B", i):
                b = i - 1
                pe.wait_ge(free["hT"], b + 1)
                for half in range(2):
                    bank = FILLS["ffn"][1][half]
                    for s in range(2):
                        t = 2 * half + s
                        m = pe.matmul(ps[:, bank, D * s:D * s + D], hT[:, P * t:P * t + P], w_up[:, :],
                                      start=False, stop=True, skip_group_check=True)
                    m.then_inc(full["ffn"], 1)
            if active("C", i):
                b = i - 2
                pe.wait_ge(free["num"], KT * (b + 1))
                transposes("y2T", y2, i)
            if active("C", i):
                b = i - 2
                pe.wait_ge(free["y2T"], 2 * b + 2)
                two_per_bank("proj", y2T, w_proj, i)

        iterations(pe, body, 1)

    @block.scalar
    def _(act):
        def evacuate(name, dst, i):
            b = i - BEHIND[FILLS[name][0]]
            for k in range(KC):
                act.wait_ge(full[name], KC * b + k + 1)
                act.copy(dst(b, k), ps[:, FILLS[name][1][k], :]).then_inc(free[name], 1)

        def positive(n, b, src, dst):
            act.wait_ge(neg_done[n], b + 1)
            act.activation(dst[:, :, :], src[:, :, :], ACT.Exp).then_inc(exp_done[n], 1)

        def inverse_std(s, b):
            act.wait_ge(mv_done[s], b + 1)
            act.activation(lnv[s][:, :], mean_var[s][:, :, 1], ACT.Ln, bias=eps[:, 0:1]).then_inc(ln_done[s], 1)
            act.wait_ge(ln_done[s], b + 1)
            act.activation(rstd[s][:, :], lnv[s][:, :], ACT.Exp, scale=-0.5).then_inc(rstd_done[s], 1)

        def gate_exponential(s, b):
            act.wait_ge(gate_step[s], GSTEPS[s] * b + 2)
            act.activation(gate[s]["ex"][:, :, :], gate[s]["shift"][:, :, :], ACT.Exp).then_inc(gate_exp[s], 1)

        def x3T_copy(i, k):
            b = i - 3
            act.wait_ge(full["x3T"], KC * b + k + 1)
            if not (isinstance(b, int) and b == 0):
                act.wait_ge(full["route"], b)
            act.copy(x3T[:, k, :], ps[:, FILLS["x3T"][1][k], :]).then_inc(free["x3T"], 1)

        def body(i):
            if active("C", i):
                b = i - 2
                for k in range(KC):
                    act.wait_ge(full["x2T"], KC * b + k + 1)
                    act.copy(x2hi[:, k, :], ps[:, FILLS["x2T"][1][k], :]).then_inc(x2hi_done, 1)
            if active("B", i):
                evacuate("x1T", lambda b, k: x1T[:, k, :], i)
            if active("A", i):
                evacuate("yT", lambda b, k: yT[:, k, :], i)
            if active("D", i):
                inverse_std("C", i - 3)
            if active("C", i):
                b = i - 2
                positive("q", b, q_neg, q_exp)
                for t in range(KT):
                    act.wait_ge(full["kv"], KT * b + t + 1)
                    act.copy(v1[:, t, :, 0:P], ps[:, FILLS["kv"][1][t], D:2 * D].rearrange("p (c f) -> p c f", c=KC)).then_inc(v_done, 1)
            if active("D", i):
                x3T_copy(i, 0)
                x3T_copy(i, 1)
            if active("C", i):
                positive("k", i - 2, k_neg, k_neg)
            if active("A", i):
                inverse_std("A", i)
            if active("B", i):
                gate_exponential("B", i - 1)
            if active("D", i):
                gate_exponential("D", i - 3)
            if active("B", i):
                b = i - 1
                act.wait_ge(full["hT"], b + 1)
                act.copy(hT[:, :], ps[0:NA, FILLS["hT"][1][0], :]).then_inc(free["hT"], 1)
            if active("C", i):
                evacuate("y2T", lambda b, k: y2T[:, k, :], i)
            if active("B", i):
                inverse_std("B", i - 1)

        act.preload_act_table_set("natural_log_exp_and_others")
        act.wait_ge(ones_set, 4)
        iterations(act, body, None)

    @block.vector
    def _(dve):
        def carry_waits():
            dve.sem_inc(waits_carried, 1)

        def phi(name, n, b, banks, neg, ex, out, w):
            src = ps[:, banks[0]:banks[-1] + 1, 0:w]
            dve.wait_ge(full[name], len(banks) * (b + 1))
            if name == "kv":
                dve.wait_ge(v_done, KT * (b + 1))
            dve.tensor_scalar(neg[:, :, :], src, 0.0, None, ALU.min).then_inc(neg_done[n], 1)
            dve.wait_ge(exp_done[n], b + 1)
            dve.scalar_tensor_tensor(out[:, :, :], src, 0.0, ex[:, :, :], ALU.max, ALU.add).then_inc(free[name], len(banks))

        def sum_up(s, b):
            name = RESIDUAL[s]
            dve.wait_ge(xb_done[s], b + 1)
            for half in range(2):
                dve.wait_ge(full[name], 2 * b + half + 1)
                dve.tensor_tensor(res[s][:, 2 * half:2 * half + 2, :],
                                  ps[:, FILLS[name][1][half], :].rearrange("p (t d) -> p t d", t=2),
                                  xb[s][:, 2 * half:2 * half + 2, :], ALU.add).then_inc(res_done[s], 1)
            for t in range(KT):
                dve.wait_ge(res_done[s], 2 * b + t // 2 + 1)
                dve.bn_stats(stats[s][:, t, :], res[s][:, t, :]).then_inc(stats_done[s], 1)
            for t in range(KT):
                dve.wait_ge(stats_done[s], KT * b + t + 1)
                carry_waits()
                m = dve.bn_aggr(mean_var[s][:, t, :], stats[s][:, t, :])
            m.then_inc(mv_done[s], 1)

        def normalise(s, b):
            dve.wait_ge(mv_done[s], b + 1)
            dve.wait_ge(rstd_done[s], b + 1)
            if not (isinstance(b, int) and b == 0):
                dve.wait_ge(full[{"A": "x1T", "B": "x2T", "C": "x3T"}[s]], KC * b)
                if s == "C":
                    dve.wait_ge(x3_out, 16 * b)
                else:
                    dve.wait_ge(xb_done[{"A": "B", "B": "C"}[s]], b)
            for t in range(KT):
                m = dve.tensor_scalar(x[s][:, t, :], res[s][:, t, :], mean_var[s][:, t, 0:1], rstd[s][:, t:t + 1],
                                      ALU.subtract, ALU.mult)
            m.then_inc(x_done[s], 1)

        def gates(i, meanwhile):
            on = [s for s in "BD" if active(s, i)]
            row = {s: i - BEHIND[s] for s in on}
            name = {"B": "lora", "D": "route"}
            lora = ps[:, FILLS["lora"][1][0], :].rearrange("p (t c) -> p t c", t=KT)
            logits = {"B": lora[:, :, NA:NA + E0],
                      "D": ps[:, FILLS["route"][1][0], 0:KT * E1].rearrange("p (t e) -> p t e", t=KT)}
            bias, n = {"B": b_route0, "D": b_route1}, {"B": E0, "D": E1}

            def pick(s, k):
                return picks[k][:, bass.ds(KT * row[s], KT), :] if s == "D" else gate[s][f"pick{k}"][:, :, :]

            def per_token(t):
                return t.to_broadcast((P, KT, E1))

            def after(s, k):
                dve.wait_ge(gate_step[s], GSTEPS[s] * row[s] + k)

            for s in on:
                dve.wait_ge(full[name[s]], row[s] + 1)
                if s == "B":
                    if not (isinstance(row[s], int) and row[s] == 0):
                        dve.wait_ge(full["hT"], row[s])
                    dve.tensor_copy(hid[:, :, :], lora[:, :, 0:NA])
                dve.tensor_tensor(gate[s]["logit"][:, :, 0:n[s]], logits[s], bias[s][:, :, :].to_broadcast((P, KT, n[s])),
                                  ALU.add).then_inc(free[name[s]], 1)
            for s in on:
                dve.wait_ge(free[name[s]], row[s] + 1)
                carry_waits()
                for t in range(KT):
                    m = dve.max(gate[s]["top"][:, t, :], gate[s]["logit"][:, t, :])
                m.then_inc(gate_step[s], 1)
            for s in on:
                after(s, 1)
                dve.tensor_tensor(gate[s]["shift"][:, :, :], gate[s]["logit"][:, :, :],
                                  per_token(gate[s]["top"][:, :, 0:1]), ALU.subtract).then_inc(gate_step[s], 1)
            for s in on:
                for t in range(KT):
                    m = dve.max_index(gate_idx[s][:, t, :], gate[s]["top"][:, t, :], gate[s]["logit"][:, t, :])
                m.then_inc(gate_step[s], 1)
            meanwhile()
            for s in on:
                after(s, 3)
                dve.tensor_copy(gate_idf[s][:, :, :], gate_idx[s][:, :, 0:2]).then_inc(gate_step[s], 1)
            for k in range(2):
                for s in on:
                    after(s, 4)
                    dve.tensor_tensor(pick(s, k), lane[:, :, :].to_broadcast((P, KT, E1)),
                                      per_token(gate_idf[s][:, :, k:k + 1]), ALU.is_equal).then_inc(gate_step[s], 1)
            for s in on:
                after(s, 6)
                dve.tensor_tensor(gate[s]["mask"][:, :, :], pick(s, 0), pick(s, 1), ALU.add).then_inc(gate_step[s], 1)
            for s in on:
                after(s, 7)
                dve.wait_ge(gate_exp[s], row[s] + 1)
                dve.tensor_tensor(gate[s]["kept"][:, :, :], gate[s]["ex"][:, :, :], gate[s]["mask"][:, :, :],
                                  ALU.mult).then_inc(gate_step[s], 1)
            for s in on:
                dve.tensor_reduce(gate_sum[s][:, :, 0], gate[s]["ex"][:, :, :], AX.X, ALU.add).then_inc(gate_step[s], 1)
            if "B" in on:
                after("B", 8)
                dve.tensor_reduce(gate_sum["B"][:, :, 1], gate["B"]["kept"][:, :, :], AX.X, ALU.add).then_inc(gate_step["B"], 1)
                after("B", 10)
                dve.scalar_tensor_tensor(gate_sum["B"][:, :, 2], gate_sum["B"][:, :, 0], 1e-6, gate_sum["B"][:, :, 1],
                                         ALU.mult, ALU.add).then_inc(gate_step["B"], 1)
            for s in on:
                after(s, GSTEPS[s] - 2)
                dve.reciprocal(gate_sum[s][:, :, 3], gate_sum[s][:, :, 2 if s == "B" else 0]).then_inc(gate_step[s], 1)
            for s in on:
                after(s, GSTEPS[s] - 1)
                out = gate["B"]["w"][:, :, :] if s == "B" else gates_all[:, bass.ds(KT * row[s], KT), :]
                dve.tensor_tensor(out, gate[s]["kept"][:, :, :], per_token(gate_sum[s][:, :, 3:4]),
                                  ALU.mult).then_inc(gate_step[s], 1)
            if "B" in on:
                after("B", GSTEPS["B"])
                dve.tensor_tensor(hid[:, :, R0:NA].rearrange("p t (e r) -> p t e r", e=E0),
                                  hid[:, :, R0:NA].rearrange("p t (e r) -> p t e r", e=E0),
                                  gate["B"]["w"][:, :, 0:E0].rearrange("p t (e o) -> p t e o", o=1).to_broadcast((P, KT, E0, R0)),
                                  ALU.mult).then_inc(hid_done, 1)

        def state_copy(i):
            if active("C", i):
                dve.wait_ge(full["state"], i - 1)
                src = ps[:, FILLS["state"][1][0], :].rearrange("p (c f) -> p c f", c=KC)
                dve.tensor_tensor(kv_bd[:, :, 0:P], src[:, :, 0:P], blocks[:, :, 0:P].to_broadcast((P, KC, P)), ALU.mult)
                dve.tensor_tensor(kv_bd[:, :, P:NB], src[:, :, P:P + 1].to_broadcast((P, KC, G)),
                                  blocks[:, :, P:NB].to_broadcast((P, KC, G)), ALU.mult).then_inc(free["state"], 1)

        def body(i):
            if isinstance(i, int) and i == 1:
                for k in range(KC):
                    dve.tensor_copy(w_hi[:, k, :], w_stage[k]).then_inc(w_parts, 1)
                for k in range(KC):
                    dve.wait_ge(w_parts, k + 1)
                    dve.tensor_tensor(w_lo[:, k, :], w_stage[k], w_hi[:, k, :], ALU.subtract).then_inc(w_parts, 1)
            if isinstance(i, int) and i == 2:
                dve.wait_ge(w_parts, 2 * KC)
            if active("C", i):
                b = i - 2
                for k in range(KC):
                    dve.wait_ge(x2hi_done, KC * b + k + 1)
                    dve.tensor_tensor(x2lo[:, k, :], ps[:, FILLS["x2T"][1][k], :], x2hi[:, k, :],
                                      ALU.subtract).then_inc(free["x2T"], 1)
            if active("D", i):
                normalise("C", i - 3)
            if active("C", i):
                b = i - 2
                phi("q", "q", b, FILLS["q"][1], q_neg, q_exp, q_phi, L)
                phi("kv", "k", b, FILLS["kv"][1], k_neg, k_neg, k_phi, D)
            if active("A", i):
                sum_up("A", i)
            gates(i, lambda: state_copy(i))
            if active("A", i):
                normalise("A", i)
            if active("C", i):
                b = i - 2
                dve.wait_ge(full["num"], KT * (b + 1))
                num = ps[:, 2:6, 0:KC * NB].rearrange("p t (c f) -> p t c f", c=KC)
                dve.reciprocal(rden[:, :, :, :], num[:, :, :, P:NB]).then_inc(rden_done, 1)
                dve.wait_ge(rden_done, b + 1)
                if not (isinstance(b, int) and b == 0):
                    dve.wait_ge(full["y2T"], 2 * b)
                for t in range(KT):
                    m = dve.tensor_tensor(y2[:, t, :].rearrange("p (c h d) -> p c h d", c=KC, h=G),
                                          num[:, t, :, 0:P].rearrange("p c (h d) -> p c h d", h=G),
                                          rden[:, t, :, :].rearrange("p c (h o) -> p c h o", o=1).to_broadcast((P, KC, G, HD)),
                                          ALU.mult)
                    m.then_inc(free["num"], 1)
            if active("B", i):
                sum_up("B", i - 1)
                normalise("B", i - 1)
            if active("C", i):
                sum_up("C", i - 2)

        dve.wait_ge(ones_set, 4)
        iterations(dve, body, 1)


def layout_middle(i):
    def chunks(w):
        w = np.asarray(w)
        return np.ascontiguousarray(w.reshape(KC, P, w.shape[1]).transpose(1, 0, 2))

    n = {k: np.asarray(v) for k, v in i.items()}
    lora = np.concatenate([n["L0_ffn_shared_A"], n["L0_ffn_routed_A"].reshape(E0 * R0, D), n["L0_ffn_router_W"]]).T
    up = np.concatenate([n["L0_ffn_shared_B"].T, n["L0_ffn_routed_B"].transpose(0, 2, 1).reshape(E0 * R0, D)])
    f = np.arange(P)
    blocks = np.concatenate([f[:, None] // HD == f[None] // HD, f[:, None] // HD == np.arange(G)[None]], 1)
    return {
        "w_out": chunks(n["L0_attn_Wout"]), "w_lora": chunks(lora), "w_base": chunks(n["L0_ffn_base_W"].T),
        "w_up": np.ascontiguousarray(up), "w_qkv1": chunks(n["L1_attn_w_qkv"]), "w_proj": chunks(n["L1_attn_w_proj"]),
        "w_route": chunks(n["L1_ffn_router_w"]), "b_out": n["L0_attn_bout"][None, None], "b_base": n["L0_ffn_base_b"][None, None],
        "b_proj": n["L1_attn_b_proj"][None, None], "b_route0": n["L0_ffn_router_b"][None, None],
        "b_route1": n["L1_ffn_router_b"][None, None], "blocks": blocks.astype(np.float32)[:, None],
        "lane": np.ascontiguousarray(np.broadcast_to(np.arange(E1, dtype=np.float32), (1, 1, E1))),
    }

FC = F1 // P
TT = B * KT
TOP = 2
BITS = E1.bit_length() - 1
ROUTED = TOP * TT + E1
HEAD = TT // 2
TILES = TT + ROUTED
PAIRS = TILES // 2
R0P, R1P = HEAD // 2, (HEAD + ROUTED) // 2
GROUP = 4


def expert_phase(nc, ctx, block_ctx, a, ident, w1, w2, gates_all, picks, x3_dram, slots_dram, y_dram, zero_done, w_in,
                 below, tile_no, sort_in, out):
    def sb(name, shape, dt=F32):
        return ctx.enter_context(nc.sbuf_tensor(name, shape, dt))

    def sem(name):
        return ctx.enter_context(nc.semaphore(name))

    b1 = sb("b1", [P, E1 + 1, F1])
    b2 = sb("b2", [P, E1 + 1, D])
    ones = sb("ones", [P, P])
    x3 = sb("x3_all", [P, TT, D])
    acc = sb("acc", [P, TT, D])
    mask = sb("mask", [P, TT, E1])
    total = sb("total", [P, TT, E1])
    scan = sb("scan", [P, 2, TT, E1])
    where = sb("where", [P, TT, E1])
    chosen = sb("chosen", [P, TOP, TT, E1])
    slot_f = sb("slot_f", [P, TOP, TT])
    slot = sb("slot", [P, TOP, TT], I32)
    count_i = sb("count_i", [P, 2, E1], I32)
    count_f = sb("count_f", [P, 2, E1])
    ends = sb("ends", [P, 2, 1, E1])
    past = sb("past", [1, ROUTED, E1])
    tile_f = sb("tile_f", [1, 2, ROUTED])
    couple = sb("couple", [1, ROUTED // 2 + 3])
    triple = sb("triple", [1, ROUTED // 2 + 1])
    near_experts = sb("near_experts", [1, ROUTED // 2 + 1], I32)
    xrow = sb("xrow", [P, 2, D])
    xT = sb("xT3", [P, KC, P])
    pre = sb("pre", [P, F1])
    hid = sb("hid3", [P, F1])
    hT = sb("hT3", [P, FC, P])
    yrow = sb("yrow", [P, 2, D])
    got = sb("got", [P, GROUP, TOP, D])
    mix = sb("mix", [P, GROUP, D])
    stats = sb("stats3", [P, GROUP, 6])
    mv = sb("mv3", [P, GROUP, 2])
    lnv = sb("lnv3", [P, GROUP])
    rstd = sb("rstd3", [P, GROUP])
    eps = sb("eps3", [P, 1])
    result = sb("result", [P, GROUP, D])
    weights_k = sb("weights_k", [P, TOP, TT])

    ps_x = ctx.enter_context(nc.psum_tensor("ps_x", [P, L], F32))
    ps_up = ctx.enter_context(nc.psum_tensor("ps_up", [P, 2, F1], F32))
    ps_h = ctx.enter_context(nc.psum_tensor("ps_h", [P, 2, F1], F32))
    ps_y = ctx.enter_context(nc.psum_tensor("ps_y", [P, 2, L], F32))
    ps_r = ctx.enter_context(nc.psum_tensor("ps_r", [P, 2, TT, E1], F32))

    shared_in = sem("e_shared_in")
    acc_ready = sem("e_acc_ready")
    tables_in = sem("e_tables_in")
    x3_in = sem("e_x3_in")
    set_up = sem("e_set_up")
    route = sem("e_route_step")
    ranks_full = sem("e_ranks_full")
    places = sem("e_places_done")
    table_done = sem("e_table_done")
    scattered = sem("e_scattered")
    x_in = [sem(f"e_x_in{p}") for p in range(2)]
    x_full = sem("e_x_full")
    x_free = sem("e_x_free")
    up_full = sem("e_up_full")
    up_free = sem("e_up_free")
    gelu_done = sem("e_gelu_done")
    h_full = sem("e_h_full")
    h_free = sem("e_h_free")
    y_full = sem("e_y_full")
    y_free = sem("e_y_free")
    y_half = sem("e_y_half")
    y_out = [sem(f"e_y_out{p}") for p in range(2)]
    gathered = [sem(f"e_gathered{t}") for t in range(GROUP)]
    mixed0 = sem("e_mixed0")
    mixed = sem("e_mixed")
    stats_done = sem("e_stats_done")
    mv_done = sem("e_mv_done")
    ln_done = sem("e_ln_done")
    rstd_done = sem("e_rstd_done")
    result_done = sem("e_result_done")
    result_out = sem("e_result_out")
    waits_carried = sem("e_waits_carried")

    block = block_ctx.enter_context(nc.Block())

    def routed(n):
        return HEAD <= n < HEAD + ROUTED

    def kind(p, lag):
        n = 2 * p - lag
        return None if n < 0 or n >= TILES else routed(n)

    def experts(eng, p, q):
        which = [routed(2 * q - 2 + k) for k in range(6)]
        if any(which[:4]):
            if q == R0P:
                eng.wait_ge(table_done, 1)
            word = eng.value_load(near_experts[0:1, bass.ds(p - R0P, 1)], min_val=0, max_val=E1 ** 6 - 1)
        else:
            which = [False] * 6
        return [((word >> (BITS * k)) & (E1 - 1)) if r else E1 for k, r in enumerate(which)]

    def pairs(eng, body, reads_table=False):
        def single(p, q):
            body(p, q, experts(eng, p, q)[:4] if reads_table else None)

        single(0, 0)
        single(1, 1)
        with eng.Fori(2, R0P) as p:
            single(p, 2)
        single(R0P, R0P)
        single(R0P + 1, R0P + 1)
        assert (R1P - R0P) % 2 == 0
        with eng.Fori(R0P // 2 + 1, R1P // 2) as m:
            p = 2 * m
            of_tile = experts(eng, p, R0P + 2) if reads_table else [None] * 6
            body(p, R0P + 2, of_tile[:4])
            body(p + 1, R0P + 2, of_tile[2:])
        single(R1P, R1P)
        single(R1P + 1, R1P + 1)
        with eng.Fori(R1P + 2, PAIRS - 1) as p:
            single(p, R1P + 2)
        single(PAIRS - 1, PAIRS - 1)
        single(PAIRS, PAIRS)

    @block.sync
    def _(sp):

        def x_load(par, src):
            sp.dma_start(xrow[:, par, :], src).then_inc(x_in[par], 16)

        def row_tile(t):
            return x3_dram[bass.ds(t * P, P), :]

        for par in range(2):
            x_load(par, row_tile(par))
        sp.dma_start(b1[:, E1:, :], a["sb1"].to_broadcast((P, 1, F1))).then_inc(shared_in, 16)
        sp.dma_start(b2[:, E1:, :], a["sb2"].to_broadcast((P, 1, D))).then_inc(shared_in, 16)

        def x3_load(c):
            sp.dma_start(x3[:, bass.ds(GROUP * c, GROUP), :],
                         x3_dram.rearrange("(i p) d -> p i d", p=P)[:, bass.ds(GROUP * c, GROUP), :]).then_inc(x3_in, 16)

        x3_load(0)

        def loads(p, to_routed, base):
            for par in range(2):
                sp.wait_ge(x_full, 2 * p + par + 1)
                n = 2 * p + 2 + par
                src = slots_dram[bass.ds((n - HEAD) * P, P), :] if to_routed else x3_dram[bass.ds((n - base) * P, P), :]
                x_load(par, src)

        def stores(p):
            for par in range(2):
                n = 2 * p + par
                sp.wait_ge(y_free, n + 1)
                sp.dma_start(y_dram[bass.ds((n - HEAD) * P, P), :], yrow[:, par, :]).then_inc(y_out[par], 16)

        def result_store(g):
            sp.wait_ge(result_done, g + 1)
            sp.dma_start(out[bass.ds(g, 1)].rearrange("g t p d -> p (g t) d"), result[:, :, :]).then_inc(result_out, 16)

        def head_loads(p):
            loads(p, False, 0)
            sp.wait_ge(x3_in, 16 * (p + 1))
            x3_load(p + 1)

        assert TT // GROUP == R0P
        with sp.Fori(0, R0P // 2 - 1) as p:
            head_loads(p)
        sp.dma_start(b1[:, 0:E1, :], a["rb1"].to_broadcast((P, E1, F1))).then_inc(tables_in, 16)
        sp.dma_start(b2[:, 0:E1, :], a["rb2"].to_broadcast((P, E1, D))).then_inc(tables_in, 16)
        with sp.Fori(R0P // 2 - 1, R0P - 1) as p:
            head_loads(p)
        sp.wait_ge(scattered, 16 * TOP * TT)
        loads(R0P - 1, True, 0)
        loads(R0P, True, 0)
        with sp.Fori(R0P + 1, R1P - 1) as p:
            loads(p, True, 0)
            stores(p - 1)
        loads(R1P - 1, False, ROUTED)
        stores(R1P - 2)
        loads(R1P, False, ROUTED)
        stores(R1P - 1)
        loads(R1P + 1, False, ROUTED)
        with sp.Fori(R1P + 2, PAIRS - 1) as p:
            loads(p, False, ROUTED)
            result_store(p - (R1P + 2))
        for g in range(PAIRS - R1P - 3, PAIRS - R1P):
            result_store(g)
        sp.wait_ge(result_out, 16 * (TT // GROUP))

    @block.gpsimd
    def _(pool):
        pool.memset(ones[:, :], 1.0).then_inc(set_up, 1)
        pool.memset(eps[:, :], LN_EPS).then_inc(set_up, 1)
        pool.wait_ge(places, 1)
        pool.wait_ge(zero_done, 16 * B)
        for i in range(TT):
            if i % GROUP == 0:
                pool.wait_ge(x3_in, 16 * (i // GROUP + 1))
            for k in range(TOP):
                pool.indirect_dma_start(slots_dram, bass.IndirectOffsetOnAxis(ap=slot[:, k, i:i + 1], axis=0),
                                        x3[:, i, :], None).then_inc(scattered, 16)
        pool.wait_ge(shared_in, 32)
        pool.tensor_tensor(acc[:, HEAD:, :], x3[:, HEAD:, :], b2[:, E1:, :].to_broadcast((P, TT - HEAD, D)),
                           ALU.add).then_inc(acc_ready, 1)
        for par in range(2):
            pool.wait_ge(y_out[par], 16 * (ROUTED // 2))
        for i in range(TT):
            g, t = i // GROUP, i % GROUP
            if g:
                pool.wait_ge(mixed, i - GROUP + 1)
            for k in range(TOP):
                pool.indirect_dma_start(got[:, t, k, :], None, y_dram,
                                        bass.IndirectOffsetOnAxis(ap=slot[:, k, i:i + 1], axis=0)).then_inc(gathered[t], 16)

    @block.tensor
    def _(pe):
        def transpose_x(n, par, half):
            pe.wait_ge(x_in[par], 16 * (half + 1))
            if not (isinstance(n, int) and n == 0):
                pe.wait_ge(x_free, n)
            for k in range(KC):
                m = pe.transpose(ps_x[:, P * k:P * k + P], xrow[:, par, P * k:P * k + P], ident[:, :])
            m.then_inc(x_full, 1)

        def up(n, par, e):
            pe.wait_ge(x_free, n + 1)
            if not (isinstance(n, int) and n < 2):
                pe.wait_ge(up_free, n - 1)
            for k in range(KC):
                m = pe.matmul(ps_up[:, par, :], xT[:, k, :], w1[:, e, k, :], start=k == 0, stop=k == KC - 1)
            m.then_inc(up_full, 1)

        def transpose_h(n, par):
            pe.wait_ge(gelu_done, n + 1)
            if not (isinstance(n, int) and n < 2):
                pe.wait_ge(h_free, n - 1)
            for c in range(FC):
                m = pe.transpose(ps_h[:, par, P * c:P * c + P], hid[:, P * c:P * c + P], ident[:, :])
            m.then_inc(h_full, 1)

        def down(n, par, e):
            pe.wait_ge(h_free, n + 1)
            if not (isinstance(n, int) and n < 2):
                pe.wait_ge(y_free, n - 1)
            for c in range(FC):
                m = pe.matmul(ps_y[:, par, 0:D], hT[:, c, :], w2[:, e, c, :], start=c == 0, stop=c == FC - 1)
            m.then_inc(y_full, 1)

        def body(p, q, of_tile):
            for par in range(2):
                n, nq = 2 * p + par, 2 * q + par
                if kind(q, 0) is not None:
                    up(n, par, of_tile[2 + par])
                if nq + 1 < TILES:
                    transpose_x(n + 1, (par + 1) % 2, p + par)
                if kind(q, 2) is not None:
                    down(n - 2, par, of_tile[par])
                if 0 <= nq - 1 < TILES:
                    transpose_h(n - 1, (par + 1) % 2)

        pe.wait_ge(w_in, 64)
        pe.wait_ge(set_up, 2)
        pe.wait_ge(sort_in, 32)
        for k, lhsT in enumerate((below, ones)):
            pe.wait_ge(route, 1)
            m = pe.matmul(ps_r[:, k, :, :], lhsT[:, :], mask[:, :, :], start=True, stop=True)
        m.then_inc(ranks_full, 1)
        transpose_x(0, 0, 0)

        pairs(pe, body, reads_table=True)

    @block.scalar
    def _(act):
        def inverse_std(g):
            act.preload_act_table_set("natural_log_exp_and_others")
            act.wait_ge(mv_done, g + 1)
            act.activation(lnv[:, :], mv[:, :, 1], ACT.Ln, bias=eps[:, 0:1]).then_inc(ln_done, 1)
            act.wait_ge(ln_done, g + 1)
            act.activation(rstd[:, :], lnv[:, :], ACT.Exp, scale=-0.5).then_inc(rstd_done, 1)

        def x_copy(n):
            act.wait_ge(x_full, n + 1)
            if not (isinstance(n, int) and n == 0):
                act.wait_ge(up_full, n)
            act.copy(xT[:, :, :], ps_x[:, 0:D].rearrange("p (k t) -> p k t", k=KC)).then_inc(x_free, 1)

        def gelu(n):
            act.wait_ge(up_free, n + 1)
            if not (isinstance(n, int) and n == 0):
                act.wait_ge(h_full, n)
            act.activation(hid[:, :], pre[:, :], ACT.Gelu).then_inc(gelu_done, 1)

        def h_copy(n, par):
            act.wait_ge(h_full, n + 1)
            if not (isinstance(n, int) and n == 0):
                act.wait_ge(y_full, n)
            act.copy(hT[:, :, :], ps_h[:, par, :].rearrange("p (c t) -> p c t", c=FC)).then_inc(h_free, 1)

        def body(p, q, of_tile):
            for par in range(2):
                n, nq = 2 * p + par, 2 * q + par
                if nq + 1 < TILES:
                    x_copy(n + 1)
                if 0 <= nq - 1 < TILES:
                    h_copy(n - 1, (par + 1) % 2)
                if nq < TILES:
                    gelu(n)
            if q > R1P:
                inverse_std(p - (R1P + 1))

        act.wait_ge(set_up, 2)
        x_copy(0)
        pairs(act, body)

    @block.vector
    def _(dve):
        step = [0]

        def link(m):
            step[0] += 1
            m.then_inc(route, 1)
            dve.wait_ge(route, step[0])

        def routing():
            link(dve.tensor_tensor(mask[:, :, :], picks[0][:, :, :], picks[1][:, :, :], ALU.add))
            dve.wait_ge(ranks_full, 1)
            link(dve.tensor_copy(total[:, :, :], ps_r[:, 1, :, :]))
            src, d, k = total[:, :, :], 1, 0
            while d < TT:
                dst = scan[:, k, :, :]
                dve.tensor_copy(dst[:, 0:d, :], src[:, 0:d, :])
                link(dve.tensor_tensor(dst[:, d:TT, :], src[:, d:TT, :], src[:, 0:TT - d, :], ALU.add))
                src, d, k = dst, 2 * d, 1 - k
            link(dve.tensor_scalar(count_i[:, 0, :], src[:, TT - 1, :], float(P - 1), None, ALU.add))
            link(dve.tensor_single_scalar(count_i[:, 1, :], count_i[:, 0, :], P.bit_length() - 1, ALU.logical_shift_right))
            link(dve.tensor_copy(count_f[:, 0, :], count_i[:, 1, :]))
            prev, d, k = count_f[:, 0, :], 1, 0
            while d < E1:
                dst = ends[:, k, 0, :]
                dve.tensor_copy(dst[:, 0:d], prev[:, 0:d])
                link(dve.tensor_tensor(dst[:, d:E1], prev[:, d:E1], prev[:, 0:E1 - d], ALU.add))
                prev, d, k = dst, 2 * d, 1 - k
            last = ends[:, 1 - k, :, :]
            link(dve.tensor_tensor(count_f[:, 1, :], prev, count_f[:, 0, :], ALU.subtract))
            link(dve.tensor_scalar(count_f[:, 1, :], count_f[:, 1, :], float(P), None, ALU.mult))
            link(dve.tensor_tensor(where[:, :, :], ps_r[:, 0, :, :], src, ALU.add))
            link(dve.tensor_tensor(where[:, :, :], where[:, :, :], total[:, :, :], ALU.subtract))
            link(dve.tensor_tensor(where[:, :, :], where[:, :, :],
                                   count_f[:, 1:2, :].to_broadcast((P, TT, E1)), ALU.add))
            for k in range(TOP):
                link(dve.tensor_tensor(chosen[:, k, :, :], where[:, :, :], picks[k][:, :, :], ALU.mult))
                link(dve.tensor_reduce(slot_f[:, k, :], chosen[:, k, :, :], AX.X, ALU.add))
            dve.tensor_copy(slot[:, :, :], slot_f[:, :, :]).then_inc(places, 1)
            return last

        def expert_table(last):
            link(dve.tensor_tensor(past[:, :, :], tile_no[:, :, :].to_broadcast((1, ROUTED, E1)),
                                   last[0:1, :, :].to_broadcast((1, ROUTED, E1)), ALU.is_ge))
            link(dve.tensor_reduce(tile_f[:, 0, :], past[:, :, :], AX.X, ALU.add))
            link(dve.tensor_scalar(tile_f[:, 1, :], tile_f[:, 0, :], float(E1 - 1), None, ALU.min))
            halves = tile_f[:, 1, :].rearrange("p (j h) -> p j h", h=2)
            link(dve.memset(couple[:, :], 0.0))
            link(dve.scalar_tensor_tensor(couple[:, 1:ROUTED // 2 + 1], halves[:, :, 1], float(E1), halves[:, :, 0],
                                          ALU.mult, ALU.add))
            n = ROUTED // 2 + 1
            link(dve.scalar_tensor_tensor(triple[:, :], couple[:, 1:n + 1], float(E1 ** 2), couple[:, 0:n], ALU.mult, ALU.add))
            dve.scalar_tensor_tensor(near_experts[:, :], couple[:, 2:n + 2], float(E1 ** 4), triple[:, :],
                                     ALU.mult, ALU.add).then_inc(table_done, 1)
            dve.wait_ge(table_done, 1)

        def add_b1(n, par, e):
            dve.wait_ge(up_full, n + 1)
            if not (isinstance(n, int) and n == 0):
                dve.wait_ge(gelu_done, n)
            dve.tensor_tensor(pre[:, :].rearrange("p (o f) -> p o f", o=1), ps_up[:, par:par + 1, :], b1[:, e, :],
                              ALU.add).then_inc(up_free, 1)

        def finish_routed(n, par, e, early):
            dve.wait_ge(y_full, n + 1)
            if not early:
                dve.wait_ge(y_out[par], 8 * (n - par - HEAD))
            dve.tensor_tensor(yrow[:, par:par + 1, :], ps_y[:, par:par + 1, 0:D], b2[:, e, :], ALU.add).then_inc(y_free, 1)

        def finish_shared(n, par, t):
            dve.wait_ge(y_full, n + 1)
            dve.tensor_tensor(yrow[:, par:par + 1, :], ps_y[:, par:par + 1, 0:D], b2[:, E1:, :], ALU.add).then_inc(y_half, 1)
            dve.wait_ge(y_half, t + 1)
            dve.tensor_tensor(acc[:, bass.ds(t, 1), :], x3[:, bass.ds(t, 1), :], yrow[:, par:par + 1, :],
                              ALU.add).then_inc(y_free, 1)

        def finish_last_shared(n, par, t):
            dve.wait_ge(y_full, n + 1)
            dve.tensor_tensor(acc[:, bass.ds(t, 1), :], ps_y[:, par:par + 1, 0:D], acc[:, bass.ds(t, 1), :],
                              ALU.add).then_inc(y_free, 1)

        def mix_half(g, half):
            if half == 0 and not (isinstance(g, int) and g == 0):
                dve.wait_ge(result_done, g)
            tiles = range(GROUP // 2 * half, GROUP // 2 * half + GROUP // 2)
            for t in tiles:
                i = GROUP * g + t
                dve.wait_ge(gathered[t], 32 * (g + 1))
                dve.scalar_tensor_tensor(mix[:, t:t + 1, :], got[:, t:t + 1, 0, :], wk(0, i), acc[:, bass.ds(i, 1), :],
                                         ALU.mult, ALU.add).then_inc(mixed0, 1)
            for t in tiles:
                i = GROUP * g + t
                dve.wait_ge(mixed0, i + 1)
                dve.scalar_tensor_tensor(mix[:, t:t + 1, :], got[:, t:t + 1, 1, :], wk(1, i), mix[:, t:t + 1, :],
                                         ALU.mult, ALU.add).then_inc(mixed, 1)

        def group_statistics(g):
            for t in range(GROUP):
                dve.wait_ge(mixed, GROUP * g + t + 1)
                dve.bn_stats(stats[:, t, :], mix[:, t, :]).then_inc(stats_done, 1)
            for t in range(GROUP):
                dve.wait_ge(stats_done, GROUP * g + t + 1)
                dve.sem_inc(waits_carried, 1)
                m = dve.bn_aggr(mv[:, t, :], stats[:, t, :])
            m.then_inc(mv_done, 1)

        def normalise_group(g):
            dve.wait_ge(mv_done, g + 1)
            dve.wait_ge(rstd_done, g + 1)
            if not (isinstance(g, int) and g == 0):
                dve.wait_ge(result_out, 16 * g)
            for t in range(GROUP):
                m = dve.tensor_scalar(result[:, t, :], mix[:, t, :], mv[:, t, 0:1], rstd[:, t:t + 1], ALU.subtract, ALU.mult)
            m.then_inc(result_done, 1)

        def wk(k, i):
            return weights_k[:, k, bass.ds(i, 1)]


        def body(p, q, of_tile):
            if 1 <= q < R0P:
                dve.wait_ge(x3_in, 16 * p)
            if q == R0P:
                dve.wait_ge(tables_in, 32)
                dve.wait_ge(x3_in, 16 * (TT // GROUP))
            if q == R1P + 1:
                dve.wait_ge(acc_ready, 1)
            for par in range(2):
                n, nq = 2 * p + par, 2 * q + par
                if nq < TILES:
                    add_b1(n, par, bass.ds(of_tile[2 + par], 1))
                if nq >= 2:
                    if routed(nq - 2):
                        finish_routed(n - 2, par, bass.ds(of_tile[par], 1), nq - 2 < HEAD + 2)
                    elif nq - 2 < HEAD:
                        finish_shared(n - 2, par, n - 2)
                    else:
                        finish_last_shared(n - 2, par, n - 2 - ROUTED)
                if q > R1P + 1 and par == 0:
                    normalise_group(p - (R1P + 2))
                if q > R1P:
                    if q == PAIRS:
                        dve.wait_ge(y_free, TILES - 1 + par)
                    mix_half(p - (R1P + 1), par)
            if q > R1P:
                group_statistics(p - (R1P + 1))
            if q == PAIRS:
                normalise_group(PAIRS - (R1P + 1))
            if q == 1:
                expert_table(last)
                for k in range(TOP):
                    dve.tensor_tensor(chosen[:, k, :, :], gates_all[:, :, :], picks[k][:, :, :], ALU.mult).then_inc(places, 1)
                    dve.wait_ge(places, 2 + 2 * k)
                    dve.tensor_reduce(weights_k[:, k, :], chosen[:, k, :, :], AX.X, ALU.add).then_inc(places, 1)
                    dve.wait_ge(places, 3 + 2 * k)

        dve.wait_ge(set_up, 2)
        dve.wait_ge(sort_in, 32)
        last = routing()
        dve.wait_ge(shared_in, 32)
        pairs(dve, body, reads_table=True)


def layout_experts(i):
    n = {k: np.asarray(v) for k, v in i.items()}
    w1 = n["L1_ffn_rw1"].reshape(E1, KC, P, F1).transpose(2, 0, 1, 3)
    w2 = n["L1_ffn_rw2"].reshape(E1, FC, P, D).transpose(2, 0, 1, 3)
    return {
        "rw1": np.ascontiguousarray(w1), "rw2": np.ascontiguousarray(w2),
        "sw1": np.ascontiguousarray(n["L1_ffn_sw1"].reshape(1, KC, P, F1).transpose(2, 0, 1, 3)),
        "sw2": np.ascontiguousarray(n["L1_ffn_sw2"].reshape(1, FC, P, D).transpose(2, 0, 1, 3)),
        "rb1": n["L1_ffn_rb1"][None], "rb2": n["L1_ffn_rb2"][None], "sb1": n["L1_ffn_sb1"][None, None], "sb2": n["L1_ffn_sb2"][None, None],
        "below": np.triu(np.ones((P, P), np.float32), 1), "tile_no": np.arange(ROUTED, dtype=np.float32)[None, :, None],
    }


def build_program(nc, a, out):
    with ExitStack() as ctx:
        y_dram = nc.dram_tensor("y_scratch", (B, L, D), F32, kind="Internal").ap()
        x3_dram = nc.dram_tensor("x3_scratch", (B, L, D), F32, kind="Internal").ap()
        slots_dram = nc.dram_tensor("slots_scratch", (ROUTED * P, D), F32, kind="Internal").ap()
        routed_dram = nc.dram_tensor("routed_scratch", (ROUTED * P, D), F32, kind="Internal").ap()
        ident = ctx.enter_context(nc.sbuf_tensor("ident", [P, P], F32))
        zero_done = ctx.enter_context(nc.semaphore("zero_done"))
        experts_in = ctx.enter_context(nc.semaphore("experts_in"))
        sort_in = ctx.enter_context(nc.semaphore("sort_in"))
        with ExitStack() as mem, ExitStack() as block:
            attention_phase(nc, mem, block, a, ident, y_dram, slots_dram, zero_done)
        gates_all = ctx.enter_context(nc.sbuf_tensor("gates_all", [P, TT, E1], F32))
        picks = [ctx.enter_context(nc.sbuf_tensor(f"pick{k}_all", [P, TT, E1], F32)) for k in range(TOP)]
        w1 = ctx.enter_context(nc.sbuf_tensor("expert_w1", [P, E1 + 1, KC, F1], F32))
        w2 = ctx.enter_context(nc.sbuf_tensor("expert_w2", [P, E1 + 1, FC, D], F32))
        below = ctx.enter_context(nc.sbuf_tensor("below", [P, P], F32))
        tile_no = ctx.enter_context(nc.sbuf_tensor("tile_no", [1, ROUTED, 1], F32))
        loads_behind = [(below[:, :], a["below"], sort_in), (tile_no[:, :, :], a["tile_no"], sort_in),
                        (w1[:, E1:], a["sw1"], experts_in), (w2[:, E1:], a["sw2"], experts_in),
                        (w1[:, 0:E1], a["rw1"], experts_in), (w2[:, 0:E1], a["rw2"], experts_in)]
        with ExitStack() as mem, ExitStack() as block:
            middle_phase(nc, mem, block, a, ident, y_dram, x3_dram, gates_all, picks, loads_behind)
        with ExitStack() as mem, ExitStack() as block:
            expert_phase(nc, mem, block, a, ident, w1, w2, gates_all, picks, x3_dram.rearrange("b l d -> (b l) d"),
                         slots_dram, routed_dram, zero_done, experts_in, below, tile_no, sort_in,
                         out.rearrange("b (t p) d -> b t p d", p=P))


def kernel(**inputs):
    import numpy as _np
    import concourse.bacc as _bacc
    from concourse import mybir as _mybir
    from concourse.bass_utils import run_bass_kernel_spmd as _run

    given = {k: _np.asarray(v) for k, v in inputs.items()}
    wqk, wv, bqk, bv = layout_attention(given)
    k_rows, q_rows, near, table = alibi_constants()
    arrays = {"x": given["L0_attn_x"], "ident": _np.eye(P, dtype=_np.float32), "wqk": wqk, "wv": wv, "bqk": bqk, "bv": bv,
              "k_rows": k_rows, "q_rows": q_rows, "near": near, "table": table}
    arrays.update(layout_middle(given))
    arrays.update(layout_experts(given))
    arrays = {f"in_{k}_dram": _np.ascontiguousarray(v) for k, v in arrays.items()}

    nc = _bacc.Bacc("TRN2", target_bir_lowering=False, num_devices=1)
    a = {k[3:-5]: nc.dram_tensor(k, v.shape, _mybir.dt.from_np(v.dtype), kind="ExternalInput").ap() for k, v in arrays.items()}
    out = nc.dram_tensor("out_dram", (B, L, D), _mybir.dt.float32, kind="ExternalOutput").ap()
    build_program(nc, a, out)
    r = _run(nc, [arrays], core_ids=[0])
    return r.results[0]["out_dram"]
```
